# Optimizing a Trainium2 kernel written in Bass

```python
import numpy as np
import jax
import jax.numpy as jnp

def _softmax(x, axis=-1):
    return jax.nn.softmax(x, axis=axis)

def _gelu(x):
    return jax.nn.gelu(x, approximate=True)

def _silu(x):
    return jax.nn.silu(x)

def _sigmoid(x):
    return jax.nn.sigmoid(x)

def _layernorm(x, axis=-1, eps=1e-05):
    m = jnp.mean(x, axis=axis, keepdims=True)
    v = jnp.var(x, axis=axis, keepdims=True)
    return (x - m) / jnp.sqrt(v + eps)

def _scatter_add(tgt, idx, src, axis=0):
    return tgt.at[idx].add(src)

def _segment_sum(src, seg, n):
    return jax.ops.segment_sum(src, seg, n)
kernel_name = 'mk_xattn_ffn_d2_seqx_r4_38396b'

def setup_inputs(seed: int=0):
    np.random.seed(seed)
    _w = jnp.asarray

    def _rec_inputs():
        import jax
        import jax.numpy as jnp
        _rk = jax.random.key(seed)
        x = -0.0002928 + 1 * jax.random.normal(jax.random.fold_in(_rk, 1), (64, 128, 256), jnp.float32)
        _lenS = 128 - jax.random.randint(jax.random.fold_in(_rk, 7), (64,), 0, max(1, 128 // 4) + 1, jnp.int32)
        _lenS2 = 128 - jax.random.randint(jax.random.fold_in(_rk, 8), (64,), 0, max(1, 128 // 4) + 1, jnp.int32)
        _ctx_1024P = jax.random.normal(jax.random.fold_in(_rk, 11), (64, 16, 256), jnp.float32)
        _ctx_1024c = jax.random.dirichlet(jax.random.fold_in(_rk, 511), 0.3 * jnp.ones((16,), jnp.float32), (64, 128))
        _ctx_1024t = jnp.einsum('bsk,bkd->bsd', _ctx_1024c, _ctx_1024P)
        _ctx_1024t = _ctx_1024t * jax.lax.rsqrt(jnp.mean(jnp.square(_ctx_1024t)) + 1e-12) * 0.953939
        ctx_1024 = -1.39393e-06 + 0.999914 * (_ctx_1024t + 0.3 * jax.random.normal(jax.random.fold_in(_rk, 611), (64, 128, 256), jnp.float32))
        _validS = jnp.arange(128)[None, :] < _lenS[:, None]
        _validS2 = jnp.arange(128)[None, :] < _lenS2[:, None]
        _causal = jnp.tril(jnp.ones((128, 128), dtype=bool))
        mask_Bx1xSxS2_if1 = jnp.where(jnp.ones((64, 1, 128, 128), dtype=bool), 1, 0).astype(jnp.int32)
        return (x, ctx_1024, _lenS2, mask_Bx1xSxS2_if1)
    x, ctx_1024, _lenS2, mask_Bx1xSxS2_if1 = _rec_inputs()

    def _L0_xattn_setup():
        import jax, jax.numpy as jnp
        import numpy as np
        D_MODEL = 256
        H = 16
        D_K = D_MODEL // H
        NEG_INF = -1000000000.0
        key = jax.random.key(seed)
        ks = jax.random.split(key, 12)
        B, S = (2, 512)
        scale = 1.0 / np.sqrt(D_MODEL)
        inp = {'q': jax.random.normal(ks[0], (B, S, D_MODEL), dtype=jnp.float32), 'k': jax.random.normal(ks[1], (B, S, D_MODEL), dtype=jnp.float32), 'v': jax.random.normal(ks[2], (B, S, D_MODEL), dtype=jnp.float32), 'mask': jnp.ones((B, 1, S, S), dtype=jnp.int32), 'w_q': jax.random.normal(ks[3], (D_MODEL, D_MODEL), dtype=jnp.float32) * scale, 'b_q': jnp.zeros((D_MODEL,), dtype=jnp.float32), 'w_k': jax.random.normal(ks[4], (D_MODEL, D_MODEL), dtype=jnp.float32) * scale, 'b_k': jnp.zeros((D_MODEL,), dtype=jnp.float32), 'w_v': jax.random.normal(ks[5], (D_MODEL, D_MODEL), dtype=jnp.float32) * scale, 'b_v': jnp.zeros((D_MODEL,), dtype=jnp.float32), 'w_o': jax.random.normal(ks[6], (D_MODEL, D_MODEL), dtype=jnp.float32) * scale, 'b_o': jnp.zeros((D_MODEL,), dtype=jnp.float32)}
        return inp
    _L0_xattn_all = _L0_xattn_setup()
    _L0_xattn_in = {k: v for k, v in _L0_xattn_all.items() if k in ('w_q', 'b_q', 'w_k', 'b_k', 'w_v', 'b_v', 'w_o', 'b_o')}
    del _L0_xattn_all

    def _L0_ffn_setup():
        import jax, jax.numpy as jnp
        import numpy as np
        EPS = 1e-05

        def _quantize(W):
            gamma = jnp.mean(jnp.abs(W))
            return jnp.clip(jnp.round(W / (gamma + EPS)), -1.0, 1.0)
        key = jax.random.key(seed)
        k_x, k_w1, k_b1, k_w2, k_b2 = jax.random.split(key, 5)
        n_embd = 256
        d_ff = 4 * n_embd
        B, S = (4, 1024)
        bound1 = 1.0 / np.sqrt(n_embd)
        bound2 = 1.0 / np.sqrt(d_ff)
        x = jax.random.normal(k_x, (B, S, n_embd), dtype=jnp.float32)
        W1 = jax.random.uniform(k_w1, (d_ff, n_embd), jnp.float32, -bound1, bound1)
        b1 = jax.random.uniform(k_b1, (d_ff,), jnp.float32, -bound1, bound1)
        W2 = jax.random.uniform(k_w2, (n_embd, d_ff), jnp.float32, -bound2, bound2)
        b2 = jax.random.uniform(k_b2, (n_embd,), jnp.float32, -bound2, bound2)
        return {'x': x, 'W1': W1, 'b1': b1, 'W2': W2, 'b2': b2}
    _L0_ffn_all = _L0_ffn_setup()
    _L0_ffn_in = {k: v for k, v in _L0_ffn_all.items() if k in ('W1', 'b1', 'W2', 'b2')}
    del _L0_ffn_all

    def _L1_xattn_setup():
        import jax, jax.numpy as jnp
        import numpy as np
        import math
        NEG = -1000000.0
        key = jax.random.key(seed)
        ks = jax.random.split(key, 8)
        B, S, D = (4, 512, 256)
        std = 1.0 / math.sqrt(D)
        return {'queries': jax.random.normal(ks[0], (B, S, D), jnp.float32), 'keys': jax.random.normal(ks[1], (B, S, D), jnp.float32), 'values': jax.random.normal(ks[2], (B, S, D), jnp.float32), 'valid_len': jax.random.randint(ks[3], (B,), 1, S, dtype=jnp.int64 if jax.config.jax_enable_x64 else jnp.int32), 'W_q': jax.random.normal(ks[4], (D, D), jnp.float32) * std, 'W_k': jax.random.normal(ks[5], (D, D), jnp.float32) * std, 'W_v': jax.random.normal(ks[6], (D, D), jnp.float32) * std, 'W_o': jax.random.normal(ks[7], (D, D), jnp.float32) * std}
    _L1_xattn_all = _L1_xattn_setup()
    _L1_xattn_in = {k: v for k, v in _L1_xattn_all.items() if k in ('W_q', 'W_k', 'W_v', 'W_o')}
    del _L1_xattn_all

    def _L1_ffn_setup():
        import jax, jax.numpy as jnp
        import numpy as np
        E = 8
        D = 256
        DO = 256
        R = 64
        H = 64
        B, T = (8, 512)
        key = jax.random.key(seed)
        ks = jax.random.split(key, 12)
        s = lambda k, shape, fan: jax.random.normal(k, shape, jnp.float32) / np.sqrt(fan)
        return {'x': jax.random.normal(ks[0], (B, T, D), jnp.float32), 'W_base': s(ks[1], (D, DO), D), 'b_base': jnp.zeros((DO,), jnp.float32), 'Wd1': s(ks[2], (E, D, H), D), 'bd1': jnp.zeros((E, H), jnp.float32), 'Wd2': s(ks[3], (E, H, D), H), 'bd2': jnp.zeros((E, D), jnp.float32), 'Wa_down': s(ks[4], (E, D, R), D), 'ba_down': jnp.zeros((E, R), jnp.float32), 'Wa_up': s(ks[5], (E, R, DO), R), 'ba_up': jnp.zeros((E, DO), jnp.float32)}
    _L1_ffn_all = _L1_ffn_setup()
    _L1_ffn_in = {k: v for k, v in _L1_ffn_all.items() if k in ('W_base', 'b_base', 'Wd1', 'bd1', 'Wd2', 'bd2', 'Wa_down', 'ba_down', 'Wa_up', 'ba_up')}
    del _L1_ffn_all
    return {'x': x, 'ctx_1024': ctx_1024, '_lenS2': _lenS2, 'mask_Bx1xSxS2_if1': mask_Bx1xSxS2_if1, 'L0_xattn_w_q': _L0_xattn_in['w_q'], 'L0_xattn_b_q': _L0_xattn_in['b_q'], 'L0_xattn_w_k': _L0_xattn_in['w_k'], 'L0_xattn_b_k': _L0_xattn_in['b_k'], 'L0_xattn_w_v': _L0_xattn_in['w_v'], 'L0_xattn_b_v': _L0_xattn_in['b_v'], 'L0_xattn_w_o': _L0_xattn_in['w_o'], 'L0_xattn_b_o': _L0_xattn_in['b_o'], 'L0_ffn_W1': _L0_ffn_in['W1'], 'L0_ffn_b1': _L0_ffn_in['b1'], 'L0_ffn_W2': _L0_ffn_in['W2'], 'L0_ffn_b2': _L0_ffn_in['b2'], 'L1_xattn_W_q': _L1_xattn_in['W_q'], 'L1_xattn_W_k': _L1_xattn_in['W_k'], 'L1_xattn_W_v': _L1_xattn_in['W_v'], 'L1_xattn_W_o': _L1_xattn_in['W_o'], 'L1_ffn_W_base': _L1_ffn_in['W_base'], 'L1_ffn_b_base': _L1_ffn_in['b_base'], 'L1_ffn_Wd1': _L1_ffn_in['Wd1'], 'L1_ffn_bd1': _L1_ffn_in['bd1'], 'L1_ffn_Wd2': _L1_ffn_in['Wd2'], 'L1_ffn_bd2': _L1_ffn_in['bd2'], 'L1_ffn_Wa_down': _L1_ffn_in['Wa_down'], 'L1_ffn_ba_down': _L1_ffn_in['ba_down'], 'L1_ffn_Wa_up': _L1_ffn_in['Wa_up'], 'L1_ffn_ba_up': _L1_ffn_in['ba_up']}

def reference(x, ctx_1024, _lenS2, mask_Bx1xSxS2_if1, L0_xattn_w_q, L0_xattn_b_q, L0_xattn_w_k, L0_xattn_b_k, L0_xattn_w_v, L0_xattn_b_v, L0_xattn_w_o, L0_xattn_b_o, L0_ffn_W1, L0_ffn_b1, L0_ffn_W2, L0_ffn_b2, L1_xattn_W_q, L1_xattn_W_k, L1_xattn_W_v, L1_xattn_W_o, L1_ffn_W_base, L1_ffn_b_base, L1_ffn_Wd1, L1_ffn_bd1, L1_ffn_Wd2, L1_ffn_bd2, L1_ffn_Wa_down, L1_ffn_ba_down, L1_ffn_Wa_up, L1_ffn_ba_up):
    import jax
    import jax.numpy as jnp

    def _L0_xattn_ref(q, k, v, mask, w_q, b_q, w_k, b_k, w_v, b_v, w_o, b_o):
        import jax, jax.numpy as jnp
        import numpy as np
        D_MODEL = 256
        H = 16
        D_K = D_MODEL // H
        NEG_INF = -1000000000.0
        B, S, _ = q.shape
        query = q @ w_q + b_q
        key_p = k @ w_k + b_k
        value = v @ w_v + b_v

        def split(x):
            return x.reshape(B, S, H, D_K).transpose(0, 2, 1, 3)
        query, key_p, value = (split(query), split(key_p), split(value))
        scores = jnp.einsum('bhqd,bhkd->bhqk', query, key_p) / jnp.sqrt(jnp.asarray(D_K, dtype=query.dtype))
        scores = jnp.where(mask == 0, NEG_INF, scores)
        attn = jax.nn.softmax(scores, axis=-1)
        out = jnp.einsum('bhqk,bhkd->bhqd', attn, value)
        out = out.transpose(0, 2, 1, 3).reshape(B, S, H * D_K)
        return out @ w_o + b_o

    def _L0_ffn_ref(x, W1, b1, W2, b2):
        import jax, jax.numpy as jnp
        import numpy as np
        EPS = 1e-05

        def _quantize(W):
            gamma = jnp.mean(jnp.abs(W))
            return jnp.clip(jnp.round(W / (gamma + EPS)), -1.0, 1.0)
        Wq1 = _quantize(W1)
        Wq2 = _quantize(W2)
        h = jax.nn.relu(jnp.einsum('bsd,fd->bsf', x, Wq1) + b1)
        out = jnp.einsum('bsf,df->bsd', h, Wq2) + b2
        return out

    def _L1_xattn_ref(queries, keys, values, valid_len, W_q, W_k, W_v, W_o):
        import jax, jax.numpy as jnp
        import numpy as np
        import math
        NEG = -1000000.0
        NUM_HEADS = 16
        B, S, D = queries.shape
        hd = D // NUM_HEADS

        def split_heads(x):
            return x.reshape(B, -1, NUM_HEADS, hd).transpose(0, 2, 1, 3)
        q = split_heads(queries @ W_q.T)
        k = split_heads(keys @ W_k.T)
        v = split_heads(values @ W_v.T)
        scale = 1.0 / math.sqrt(hd)
        scores = jnp.einsum('bhqd,bhkd->bhqk', q, k) * scale
        kpos = jnp.arange(scores.shape[-1])
        pad_mask = kpos[None, None, None, :] >= valid_len[:, None, None, None]
        scores = jnp.where(pad_mask, NEG, scores)
        attn = jax.nn.softmax(scores, axis=-1)
        out = jnp.einsum('bhqk,bhkd->bhqd', attn, v)
        out = out.transpose(0, 2, 1, 3).reshape(B, -1, D)
        return out @ W_o.T

    def _L1_ffn_ref(x, W_base, b_base, Wd1, bd1, Wd2, bd2, Wa_down, ba_down, Wa_up, ba_up):
        import jax, jax.numpy as jnp
        import numpy as np
        E = 8
        D = 256
        DO = 256
        R = 64
        H = 64
        B, T = (8, 512)
        base = jnp.einsum('btd,do->bto', x, W_base) + b_base
        h = jax.nn.relu(jnp.einsum('btd,edh->ebth', x, Wd1) + bd1[:, None, None, :])
        recon = jnp.einsum('ebth,ehd->ebtd', h, Wd2) + bd2[:, None, None, :]
        losses = jnp.mean((recon - x[None]) ** 2, axis=(2, 3))
        idx = jnp.argmin(losses, axis=0)
        a = jax.nn.relu(jnp.einsum('btd,bdr->btr', x, Wa_down[idx]) + ba_down[idx][:, None, :])
        adapter_out = jnp.einsum('btr,bro->bto', a, Wa_up[idx]) + ba_up[idx][:, None, :]
        return base + adapter_out
    x = x + _L0_xattn_ref(_layernorm(x, axis=-1), ctx_1024, ctx_1024, mask_Bx1xSxS2_if1, L0_xattn_w_q, L0_xattn_b_q, L0_xattn_w_k, L0_xattn_b_k, L0_xattn_w_v, L0_xattn_b_v, L0_xattn_w_o, L0_xattn_b_o)
    x = x + _L0_ffn_ref(_layernorm(x, axis=-1), L0_ffn_W1, L0_ffn_b1, L0_ffn_W2, L0_ffn_b2)
    x = x + _L1_xattn_ref(_layernorm(x, axis=-1), ctx_1024, ctx_1024, _lenS2, L1_xattn_W_q, L1_xattn_W_k, L1_xattn_W_v, L1_xattn_W_o)
    x = x + _L1_ffn_ref(_layernorm(x, axis=-1), L1_ffn_W_base, L1_ffn_b_base, L1_ffn_Wd1, L1_ffn_bd1, L1_ffn_Wd2, L1_ffn_bd2, L1_ffn_Wa_down, L1_ffn_ba_down, L1_ffn_Wa_up, L1_ffn_ba_up)
    return x

_drawn_inputs = setup_inputs


def setup_inputs(seed=0):
    import zlib

    import numpy as np

    out = dict(_drawn_inputs(seed))
    spreads = {'L0_xattn_b_q': (0.0, 0.423),
     'L0_xattn_b_k': (0.0, 2.0),
     'L0_xattn_b_v': (0.0, 0.1),
     'L0_xattn_b_o': (0.0, 0.1),
     'L1_ffn_b_base': (0.0, 2.0),
     'L1_ffn_bd1': (0.0, 0.8),
     'L1_ffn_bd2': (0.0, 0.8),
     'L1_ffn_ba_down': (0.0, 2.0),
     'L1_ffn_ba_up': (0.0, 2.0)}
    factors = {'L0_ffn_b1': 8.0,
     'L0_ffn_b2': 183.411,
     'L1_xattn_W_q': 8.0,
     'L1_xattn_W_k': 8.0,
     'L1_xattn_W_v': 8.0,
     'L1_xattn_W_o': 8.0,
     'L1_ffn_W_base': 8.0,
     'L1_ffn_Wd1': 8.0,
     'L1_ffn_Wd2': 8.0,
     'L1_ffn_Wa_down': 8.0,
     'L1_ffn_Wa_up': 8.0}
    for name, (base, spread) in spreads.items():
        noise = np.random.default_rng([zlib.crc32(name.encode()), seed]).standard_normal(out[name].shape)
        drawn = base * np.exp(spread * noise) if base else spread * noise
        out[name] = jnp.asarray(drawn.astype(out[name].dtype))
    for name, factor in factors.items():
        out[name] = (out[name] * factor).astype(out[name].dtype)
    return out
```

```python
from contextlib import ExitStack

import numpy as np

import concourse.bass as bass
from concourse import mybir

F32 = mybir.dt.float32
F16 = mybir.dt.float16
BF16 = mybir.dt.bfloat16
I32 = mybir.dt.int32
U32 = mybir.dt.uint32
ALU = mybir.AluOpType
ACT = mybir.ActivationFunctionType
AX = mybir.AxisListType
RADD = bass.bass_isa.ReduceOp.add

P = 128
B = 64
D = 256
KD = D // P
H = 16
HD = D // H
F = 1024
KF = F // P
E = 8
R = 64
CB = 4
NC = 2
IB = CB * NC
ITERS = B // IB
CT = CB * P
UNITS = 2 * IB
UH = H // 2
PAIRS = H // 2
LAG = 3
EPS = 1e-5
HUGE = 3e38
ROUND = 1.5 * 2.0 ** 23
SCALE = 0.25
FILL = (-4e9, -4e6)


def carry(eng, tally):
    eng.sem_inc(tally, 1)


def part_index(l, c, j, m):
    return ((2 * l + 1 - j) * NC + c) * KD + m


class Signal:

    def __init__(self, sem, per):
        self.sem, self.per = sem, per

    def prime(self, eng):
        eng.sem_inc(self.sem, self.per)

    def done(self, eng, it, n):
        eng.wait_ge(self.sem, it * self.per + (self.per + n + 1))

    def past(self, eng, it, n):
        eng.wait_ge(self.sem, it * self.per + (n + 1))

    def slot(self, eng, it, n, slots):
        if n >= slots:
            self.done(eng, it, n - slots)
        else:
            self.past(eng, it, self.per + n - slots)


def build(nc, x, ctx_in, lens, mask, wq0, bq0, wk0, bk0, wv0, bv0, wo0, bo0, w1t, b1, w2t, b2,
          wq1, wk1, wv1, wo1, w_base, b_base, wd1, bd1, wd2, bd2, wa_down, ba_down, wa_up, ba_up,
          out):
    with ExitStack() as ctx:
        def sb(name, shape, dt):
            return ctx.enter_context(nc.sbuf_tensor(name, shape, dt))

        def pb(name, shape):
            return ctx.enter_context(nc.psum_tensor(name, shape, F32))

        def sem(name):
            return ctx.enter_context(nc.semaphore(name))

        wq = [sb(f"wq{l}", [P, KD, D], F32) for l in range(2)]
        wk = [sb(f"wk{l}", [P, KD, D], F32) for l in range(2)]
        wv = [sb(f"wv{l}", [P, KD, D], F32) for l in range(2)]
        wo = [sb(f"wo{l}", [P, KD, D], F32) for l in range(2)]
        w1q = sb("w1q", [P, KD, F], F16)
        w2q = sb("w2q", [P, KF, D], F16)
        wb = sb("wb", [P, KD, D], F32)
        wd1s = sb("wd1s", [P, KD, E, R], F32)
        wd2s = sb("wd2s", [P, E, D], F32)
        bqk = sb("bqk", [P, 2, 2, KD], F32)
        bvb = sb("bvb", [P, 2, D], F32)
        bob = sb("bob", [P, D], F32)
        b2b = sb("b2b", [P, D], F32)
        b1s = sb("b1s", [P, KF], F32)
        bd1s = sb("bd1s", [P, E // 2], F32)
        bd2s = sb("bd2s", [P, E, KD], F32)
        ident = sb("ident", [P, P], F32)
        sel = sb("sel", [P, 2, 2 * HD], F32)
        ones = sb("ones", [P, 1], F32)
        kpos = sb("kpos", [P, P], F32)
        mhalf = sb("mhalf", [P, CB], F32)
        lens_i = sb("lens_i", [P, B], I32)
        lens_f = sb("lens_f", [P, B], F32)
        gam = sb("gam", [P, 8], F32)

        xr = sb("xr", [P, IB, D], F32)
        ctxT = sb("ctxT", [P, NC, KD, CT], F32)
        bound = sb("bound", [P, 2, IB, P], BF16)
        xn = [sb(f"xn{c}", [P, CB, D], F32) for c in range(NC)]
        xT = [sb(f"xT{c}", [P, KD, CT], F32) for c in range(NC)]
        stats = sb("stats", [P, IB, 6], F32)
        mv = sb("mv", [P, IB, 2], F32)
        veps = sb("veps", [P, IB], F32)
        rstd = sb("rstd", [P, IB], F32)
        packed = sb("packed", [P, NC, 2, 2, KD, CT], F16)
        qst = sb("qst", [P, NC, PAIRS, CT], F16)
        kst = sb("kst", [P, NC, PAIRS, 2, CT], F16)
        v2 = sb("v2", [P, NC, CB, PAIRS, 4, HD], F32)
        sm = sb("sm", [P, 4, UH, P], F32)
        mx = sb("mx", [P, 4, UH], F32)
        pT = sb("pT", [P, 2, UH, P], F32)
        rden = sb("rden", [P, 2, 2 * P], F32)
        attT = sb("attT", [P, 2, 2 * P], F32)
        work = sb("work", [P, 2, 2, CT], F32)
        acc = sb("acc", [P, NC * CB * E], F32)
        lneg = sb("lneg", [1, NC * CB * E], F32)
        lmax = sb("lmax", [1, NC * CB, 8], F32)
        lidx = sb("lidx", [1, NC * CB, 8], U32)
        dws = sb("dws", [P, CB, KD, R], F32)
        das = sb("das", [R, CB], F32)
        ups = sb("ups", [R + 2, CB, D], F32)
        aT = sb("aT", [R + 2, CT], F32)

        ctx_ld = sm[:, 0:2].rearrange("p s h t -> p (s h t)").rearrange("p (b d) -> p b d", d=D)
        x_ld = sm[:, 2:4].rearrange("p s h t -> p (s h t)").rearrange("p (b d) -> p b d", d=D)
        mask_ld = pT[:, 0].rearrange("p h t -> p (h t)").rearrange("p (b t) -> p b t", t=P).bitcast(I32)
        xs16 = [xT[c][:].rearrange("p k t -> p (k t)").bitcast(F16)
                .rearrange("p (s k t) -> p s k t", s=2, k=KD) for c in range(NC)]
        hh = [qst[:, 0], packed[:, 0].rearrange("p a b k t -> p (a b k) t")]
        hl = [qst[:, 1], packed[:, 1].rearrange("p a b k t -> p (a b k) t")]
        hd = [packed[:, c].rearrange("p a b k t -> p (a b k t)").bitcast(F32)
              .rearrange("p (m t) -> p m t", m=E // 2) for c in range(NC)]
        w1_ld = kst[:, 0].rearrange("p a b t -> p (a b t)").bitcast(F32)[:, 0:KD * F]
        w2_ld = kst[:, 1].rearrange("p a b t -> p (a b t)").bitcast(F32)[:, 0:KF * D]

        S = [pb(f"psS{k}", [P, 1024]) for k in range(2)]
        T = [pb(f"psT{k}", [P, 512]) for k in range(2)]
        V = pb("psV", [P, 512])
        O = pb("psO", [P, 512])

        def signal(name, per):
            return Signal(sem(name), per)

        ctxT_ready = signal("ctxT_ready", NC)
        xT_ready = signal("xT_ready", 4 * NC)
        q_ready = signal("q_ready", 2 * NC)
        k_ready = signal("k_ready", 2 * NC)
        v_ready = signal("v_ready", 2 * NC)
        scores_ready = signal("scores_ready", 2 * UNITS)
        probsT_ready = signal("probsT_ready", 4 * UNITS)
        mixed_ready = signal("mixed_ready", 2 * IB)
        oproj_ready = signal("oproj_ready", 2 * IB)
        h_ready = signal("h_ready", KF)
        ffn_ready = signal("ffn_ready", NC)
        hd_ready = signal("hd_ready", 2 * NC)
        recon_ready = signal("recon_ready", NC * E)
        loss_ready = signal("loss_ready", NC)
        down_ready = signal("down_ready", NC)
        up_ready = signal("up_ready", NC)
        ctxT_copied = signal("ctxT_copied", NC)
        xT_copied = signal("xT_copied", 4 * NC)
        qk_high = signal("qk_high", 2 * NC * 2 * KD)
        exp_done = signal("exp_done", 2 * UNITS)
        probsT_copied = signal("probsT_copied", 4 * UNITS)
        h_relu = signal("h_relu", NC * KF)
        hd_relu = signal("hd_relu", NC * E // 2)
        squared = signal("squared", NC * E * CB)
        a_relu = signal("a_relu", NC * CB)
        bound_part = signal("bound_part", 2)
        bound_ready = signal("bound_ready", 2)
        stats_done = signal("stats_done", 4 * IB)
        moments = signal("moments", 4 * IB)
        normed = signal("normed", 4 * IB)
        qk_low = signal("qk_low", 2 * NC * 2 * KD)
        v_copied = signal("v_copied", 2 * IB)
        masked = signal("masked", 2 * UNITS)
        max_done = signal("max_done", 2 * UNITS)
        recip_done = signal("recip_done", 2 * IB)
        attT_ready = signal("attT_ready", 2 * IB)
        att_added = signal("att_added", 2 * IB)
        x_low = signal("x_low", NC)
        h_high = signal("h_high", KF)
        h_low = signal("h_low", KF)
        ffn_added = signal("ffn_added", NC)
        diffed = signal("diffed", NC * E * KD)
        loss_out = signal("loss_out", NC)
        best_loss = signal("best_loss", NC * CB)
        expert_found = signal("expert_found", NC * CB)
        y_ready = signal("y_ready", NC)
        veps_ready = signal("veps_ready", 4 * NC)
        rstd_ready = signal("rstd_ready", 4 * NC)
        bias_added = signal("bias_added", 2 * NC)
        shifted = signal("shifted", 2 * UNITS)
        STACK = 16 * (4 * 4 + 8 * 4)
        GATHER = 16 * 4 * CB
        x_loaded, ctx_loaded, mask_loaded = sem("x_loaded"), sem("ctx_loaded"), sem("mask_loaded")
        stacked = [sem(f"stacked{c}") for c in range(NC)]
        gathered = sem("gathered")
        stored = [sem(f"stored{c}") for c in range(NC)]
        w_loaded, ffn_w_loaded = sem("w_loaded"), sem("ffn_w_loaded")
        wd2_loaded = sem("wd2_loaded")
        consts_set, consts_ready = sem("consts_set"), sem("consts_ready")
        zeros_set, gamma_part, gamma_sum = sem("zeros_set"), sem("gamma_part"), sem("gamma_sum")
        quant, staged_free = sem("quant"), sem("staged_free")

        dve_tally, pool_tally = sem("dve_tally"), sem("pool_tally")

        xv = x.rearrange("b s d -> s b d")
        cv = ctx_in.rearrange("b s d -> s b d")
        mv_dram = mask.rearrange("b o q k -> q (b o) k")
        outv = out.rearrange("b s d -> s b d")

        def rows(w):
            return w.rearrange("(k p) n -> p k n", p=P)

        def col(b):
            return b.rearrange("(k p) -> p k", p=P)

        def everywhere(b):
            return b.rearrange("(a n) -> a n", a=1).to_broadcast([P, D])

        WEIGHTS = [(ctx_w[:], rows(src)) for ctx_w, src in (
            (wk[0], wk0), (wv[0], wv0), (wq[0], wq0), (wo[0], wo0), (wk[1], wk1), (wv[1], wv1),
            (wq[1], wq1), (wo[1], wo1), (wb, w_base))]
        WEIGHTS += [(bqk[:, 0, 0, :], col(bq0)), (bqk[:, 0, 1, :], col(bk0)),
                    (bvb[:, 0, :], everywhere(bv0)), (bob[:], everywhere(bo0)), (b2b[:], everywhere(b2)),
                    (b1s[:], col(b1)),
                    (bd1s[:], bd1.rearrange("(m e) r -> (e r) m", e=2)),
                    (lens_i[:], lens.rearrange("(a n) -> a n", a=1).to_broadcast([P, B]))]
        WEIGHTS += [(wd1s[:, k], wd1[:, P * k:P * k + P, :].rearrange("e p r -> p e r")) for k in range(KD)]
        WEIGHTS += [(bd2s[:, :, k], bd2[:, P * k:P * k + P].rearrange("e p -> p e")) for k in range(KD)]
        WEIGHTS += [(wd2s[R * s:R * s + R, s:E:2, :], wd2[s:E:2].rearrange("e r d -> r e d")) for s in range(2)]
        WEIGHTS += [(ups[R + 1:R + 2, b, :], b_base.rearrange("(a n) -> a n", a=1)) for b in range(CB)]
        N_W = len(WEIGHTS)

        N_ZEROS = 3

        block = ctx.enter_context(nc.Block())

        @block.sync
        def _(sp):
            n_ffn = 0
            for dst, src in ((w1_ld.rearrange("p (k f) -> p k f", k=KD), w1t.rearrange("(k p) f -> p k f", p=P)),
                             (w2_ld.rearrange("p (k d) -> p k d", k=KF), w2t.rearrange("(k p) d -> p k d", p=P))):
                sp.dma_start(dst, src).then_inc(ffn_w_loaded, 16)
                n_ffn += 1
            sp.wait_ge(zeros_set, N_ZEROS)
            with nc.allow_non_contiguous_dma(reason="biases, one or a few for each partition, once"):
                for dst, src in WEIGHTS:
                    sp.dma_start(dst, src).then_inc(w_loaded, 16)
            with sp.Fori(0, ITERS) as it:
                probsT_ready.past(sp, it, 4 * UNITS - 1)
                sp.dma_start(ctx_ld, cv[:, bass.ds(it * IB, IB), :]).then_inc(ctx_loaded, 16)
                sp.dma_start(x_ld, xv[:, bass.ds(it * IB, IB), :]).then_inc(x_loaded, 16)
                mixed_ready.past(sp, it, 2 * IB - 1)
                sp.dma_start(mask_ld, mv_dram[:, bass.ds(it * IB, IB), :]).then_inc(mask_loaded, 16)
                for l in range(2):
                    for c in range(NC):
                        if l == 0:
                            scores_ready.past(sp, it, UNITS + 8 * c + 7)
                        else:
                            scores_ready.done(sp, it, 8 * c + 7)
                            ffn_ready.done(sp, it, 0)
                        for j, dst in ((1, kst), (0, qst)):
                            qk_high.done(sp, it, part_index(l, c, j, KD - 1))
                            qk_low.done(sp, it, part_index(l, c, j, KD - 1))
                            hi, lo = packed[:, c, j, 0], packed[:, c, j, 1]
                            for quad in range(4):
                                src = (hi, hi, lo, lo)[quad] if j == 0 else (hi, lo, hi, lo)[quad]
                                if j == 0:
                                    for r in range(4):
                                        sp.dma_start(qst[32 * quad:32 * quad + 32, c, r:PAIRS:4, :],
                                                     src[32 * r:32 * r + 32]).then_inc(stacked[c], 16)
                                else:
                                    for r in range(8):
                                        s = r % 2
                                        sp.dma_start(
                                            kst[32 * quad + 16 * s:32 * quad + 16 * s + 16, c, r // 2:PAIRS:4, s, :],
                                            src[16 * r:16 * r + 16]).then_inc(stacked[c], 16)
            sp.wait_ge(stored[0], 16 * (ITERS + 1))
            sp.wait_ge(stored[1], 16 * (ITERS + 1))

        @block.gpsimd
        def _(pool):
            for s in (veps_ready, rstd_ready, bias_added, shifted):
                s.prime(pool)
            nc.gpsimd.memset(ident[:], 0.0).then_inc(consts_set, 1)
            nc.gpsimd.memset(sel[:], 0.0).then_inc(consts_set, 1)
            nc.gpsimd.memset(ones[:], 1.0).then_inc(consts_ready, 1)
            nc.gpsimd.memset(mhalf[:], -0.5).then_inc(consts_ready, 1)
            nc.gpsimd.iota(kpos[:], pattern=[[1, P]], base=0, channel_multiplier=0,
                           allow_small_or_imprecise_dtypes=True).then_inc(consts_ready, 1)
            pool.wait_ge(consts_set, 2)
            nc.gpsimd.affine_select(out=ident[:], in_=ident[:], compare_op=ALU.not_equal, fill=1.0,
                                    base=0, pattern=[[-1, P]], channel_multiplier=1).then_inc(consts_ready, 1)
            nc.gpsimd.memset(sel[:, 0, 0:HD], 1.0).then_inc(consts_ready, 1)
            nc.gpsimd.memset(sel[:, 1, HD:2 * HD], 1.0).then_inc(consts_ready, 1)
            for w in range(2):
                pool.wait_ge(gamma_part, w + 1)
                nc.gpsimd.partition_all_reduce(gam[:, 2 + w:3 + w], gam[:, w:w + 1], P, RADD).then_inc(gamma_sum, 1)
            pool.wait_ge(w_loaded, 16 * N_W)
            pool.wait_ge(consts_ready, 7)

            def rstd_of(it, s, c):
                moments.done(pool, it, (s * NC + c) * CB + CB - 1)
                if s:
                    normed.done(pool, it, ((s - 1) * NC + c) * CB + CB - 1)
                else:
                    normed.past(pool, it, (3 * NC + c) * CB + CB - 1)
                b0 = c * CB
                carry(pool, pool_tally)
                nc.gpsimd.tensor_scalar(veps[:, b0:b0 + CB], mv[:, b0:b0 + CB, 1], EPS, None, ALU.add)\
                    .then_inc(veps_ready.sem, 1)
                veps_ready.done(pool, it, s * NC + c)
                nc.gpsimd.tensor_tensor(rstd[:, b0:b0 + CB], veps[:, b0:b0 + CB], mhalf[:, 0:CB], ALU.pow)\
                    .then_inc(rstd_ready.sem, 1)

            with pool.Fori(0, ITERS) as it:
                pool.wait_ge(x_loaded, it * 16 + 16)
                for c in range(NC):
                    pool.wait_ge(stored[c], it * 16 + 16)
                    nc.gpsimd.tensor_tensor(xr[:, c * CB:c * CB + CB, :], x_ld[:, c * CB:c * CB + CB, :],
                                            bob[:].unsqueeze(1).to_broadcast([P, CB, D]), ALU.add)\
                        .then_inc(bias_added.sem, 1)
                    rstd_of(it, 0, c)
                for l in range(2):
                    for u in range(UNITS):
                        g = UNITS * l + u
                        max_done.done(pool, it, g)
                        nc.gpsimd.tensor_tensor(sm[:, g % 4], sm[:, g % 4],
                                                mx[:, g % 4].unsqueeze(2).to_broadcast([P, UH, P]),
                                                ALU.subtract).then_inc(shifted.sem, 1)
                    for c in range(NC):
                        rstd_of(it, 2 * l + 1, c)
                    if l == 0:
                        for c in range(NC):
                            normed.done(pool, it, (NC + c) * CB + CB - 1)
                            blk = xr[:, c * CB:c * CB + CB, :]
                            nc.gpsimd.tensor_tensor(blk, blk, b2b[:].unsqueeze(1).to_broadcast([P, CB, D]),
                                                    ALU.add).then_inc(bias_added.sem, 1)
                        for c in range(NC):
                            rstd_of(it, 2, c)
                for c in range(NC):
                    for b in range(CB):
                        expert_found.done(pool, it, c * CB + b)
                        if b == 0:
                            if c:
                                up_ready.done(pool, it, c - 1)
                            else:
                                up_ready.past(pool, it, NC - 1)
                        carry(pool, pool_tally)
                        e = pool.value_load(lidx[0:1, c * CB + b, 0:1], min_val=0, max_val=E - 1)
                        pool.dma_start(dws[:, b], wa_down[bass.ds(e, 1)].rearrange("a (k p) r -> p (a k) r", p=P))\
                            .then_inc(gathered, 16)
                        with nc.allow_non_contiguous_dma(reason="64 biases, one for each partition"):
                            pool.dma_start(das[:, b:b + 1], ba_down[bass.ds(e, 1)].rearrange("a r -> r a"))\
                                .then_inc(gathered, 16)
                        pool.dma_start(ups[0:R, b, :], wa_up[bass.ds(e, 1)].rearrange("a r d -> (a r) d"))\
                            .then_inc(gathered, 16)
                        pool.dma_start(ups[R:R + 1, b, :], ba_up[bass.ds(e, 1)]).then_inc(gathered, 16)
                pool.nop()

        @block.scalar
        def _(act):
            for s in (ctxT_copied, xT_copied, qk_high, exp_done, probsT_copied, h_relu, hd_relu,
                      squared, a_relu):
                s.prime(act)
            for c in range(NC):
                act.sem_inc(stored[c], 16)
                act.sem_inc(stacked[c], 16)
            act.wait_ge(w_loaded, 16 * N_W)

            def store(it, c):
                y_ready.done(act, it, c)
                act.dma_start(outv[:, bass.ds(it * IB + c * CB, CB), :],
                              xr[:, c * CB:c * CB + CB, :]).then_inc(stored[c], 16)

            def copy_xT(it, s, c):
                xT_ready.done(act, it, s * NC + c)
                if s == 0:
                    up_ready.past(act, it, c)
                elif s == 1:
                    q_ready.done(act, it, c)
                elif s == 2:
                    h_ready.done(act, it, 4 * c + 3)
                else:
                    q_ready.done(act, it, NC + c)
                if s == 1:
                    nc.scalar.activation(xs16[c][:, 0].rearrange("p k t -> p (k t)"), S[0][:], ACT.Copy)\
                        .then_inc(xT_copied.sem, 1)
                else:
                    nc.scalar.activation(xT[c][:].rearrange("p k t -> p (k t)"), S[0][:], ACT.Copy)\
                        .then_inc(xT_copied.sem, 1)

            def high_parts(it, l, c, j):
                (k_ready if j else q_ready).done(act, it, 2 * l + c)
                if j:
                    act.wait_ge(stacked[c], (it * 2 + l) * STACK + 16)
                    if l:
                        ffn_ready.done(act, it, 1)
                    else:
                        recon_ready.past(act, it, NC * E - 1)
                src = S[0] if j else S[1]
                for m in range(KD):
                    nc.scalar.activation(packed[:, c, j, 0, m], src[:, m * CT:m * CT + CT], ACT.Identity,
                                         bias=bqk[:, l, j, m:m + 1]).then_inc(qk_high.sem, 1)

            def attention(it, l):
                for t in range(UNITS + LAG):
                    if 2 <= t < UNITS + 2:
                        g = UNITS * l + t - 2
                        shifted.done(act, it, g)
                        nc.scalar.activation(sm[:, g % 4], sm[:, g % 4], ACT.Exp, scale=SCALE)\
                            .then_inc(exp_done.sem, 1)
                    if t >= LAG:
                        u = t - LAG
                        g = UNITS * l + u
                        if g >= 2:
                            mixed_ready.done(act, it, g // 2 - 1)
                        else:
                            mixed_ready.past(act, it, 2 * IB - 1)
                            bound_ready.done(act, it, 0)
                        for q in range(2):
                            probsT_ready.done(act, it, 2 * g + q)
                            nc.scalar.activation(pT[:, u % 2, 4 * q:4 * q + 4].rearrange("p h t -> p (h t)"),
                                                 T[q][:], ACT.Copy).then_inc(probsT_copied.sem, 1)

            with act.Fori(0, ITERS) as it:
                for c in range(NC):
                    ctxT_ready.done(act, it, c)
                    v_ready.past(act, it, 2 * NC - 1)
                    nc.scalar.activation(ctxT[:, c].rearrange("p k t -> p (k t)"), S[c][:], ACT.Copy)\
                        .then_inc(ctxT_copied.sem, 1)
                for l in range(2):
                    for c in range(NC):
                        high_parts(it, l, c, 1)
                    for c in range(NC):
                        copy_xT(it, 2 * l, c)
                        high_parts(it, l, c, 0)
                    attention(it, l)
                    if l == 0:
                        for c in range(NC):
                            copy_xT(it, 1, c)
                            for m in range(KF):
                                if m % 2 == 0:
                                    h_ready.done(act, it, (KF * c + m) // 2)
                                    if KF * c + m >= 4:
                                        h_low.done(act, it, (KF * c + m) // 2 - 2)
                                    else:
                                        squared.past(act, it, squared.per - 1)
                                nc.scalar.activation(work[:, m // 2 % 2, m % 2],
                                                     S[(m // 2 + 1) % 2][:, (m % 2) * CT:(m % 2) * CT + CT],
                                                     ACT.Relu, bias=b1s[:, m:m + 1]).then_inc(h_relu.sem, 1)
                for c in range(NC):
                    copy_xT(it, 3, c)
                    act.wait_ge(stacked[c], (it * 2 + 2) * STACK + 16)
                    for m in range(E // 2):
                        if m % 2 == 0:
                            hd_ready.done(act, it, 2 * c + m // 2)
                        nc.scalar.activation(hd[c][:, m], S[(m // 2 + 1) % 2][:, (m % 2) * CT:(m % 2) * CT + CT],
                                             ACT.Relu, bias=bd1s[:, m:m + 1]).then_inc(hd_relu.sem, 1)
                    if c == 0:
                        loss_ready.past(act, it, NC - 1)
                    for e in range(E):
                        diffed.done(act, it, (E * c + e) * KD + 1)
                        for b in range(CB):
                            blk = work[:, e % 2, :, P * b:P * b + P]
                            k = (c * CB + b) * E + e
                            nc.scalar.activation(blk, blk, ACT.Square, accum_out=acc[:, k:k + 1])\
                                .then_inc(squared.sem, 1)
                for c in range(NC):
                    down_ready.done(act, it, c)
                    if c:
                        up_ready.done(act, it, c - 1)
                    else:
                        up_ready.past(act, it, NC - 1)
                    for b in range(CB):
                        nc.scalar.activation(aT[0:R, P * b:P * b + P], T[c][0:R, P * b:P * b + P], ACT.Relu,
                                             bias=das[:, b:b + 1]).then_inc(a_relu.sem, 1)
                for c in range(NC):
                    store(it, c)

        @block.vector
        def _(dve):
            for s in (bound_part, bound_ready, stats_done, moments, normed, qk_low, v_copied, masked,
                      max_done, recip_done, attT_ready, att_added, x_low, h_high, h_low, ffn_added,
                      diffed, loss_out, best_loss, expert_found, y_ready):
                s.prime(dve)
            for z in (wd2s, bqk, bvb):
                nc.vector.memset(z[:], 0.0).then_inc(zeros_set, 1)
            nc.vector.memset(v2[:], 0.0).then_inc(quant, 1)
            nc.vector.memset(aT[R:R + 2, :], 1.0).then_inc(consts_ready, 1)
            dve.wait_ge(ffn_w_loaded, 32)
            n = 1
            for w, ld in enumerate((w1_ld, w2_ld)):
                nc.vector.tensor_reduce(gam[:, w:w + 1], ld, AX.X, ALU.add, apply_absolute_value=True)\
                    .then_inc(gamma_part, 1)
            for w, (ld, dst) in enumerate(((w1_ld, w1q), (w2_ld, w2q))):
                dve.wait_ge(gamma_sum, w + 1)
                nc.vector.tensor_scalar(gam[:, 4 + w:5 + w], gam[:, 2 + w:3 + w], 1.0 / (F * D), EPS, ALU.mult,
                                        ALU.add).then_inc(quant, 1)
                n += 1
                dve.wait_ge(quant, n)
                nc.vector.reciprocal(gam[:, 6 + w:7 + w], gam[:, 4 + w:5 + w]).then_inc(quant, 1)
                n += 1
                dve.wait_ge(quant, n)
                nc.vector.tensor_scalar(ld, ld, gam[:, 6 + w:7 + w], ROUND, ALU.mult, ALU.add).then_inc(quant, 1)
                n += 1
                dve.wait_ge(quant, n)
                nc.vector.tensor_scalar(ld, ld, ROUND, 1.0, ALU.subtract, ALU.min).then_inc(quant, 1)
                n += 1
                dve.wait_ge(quant, n)
                nc.vector.tensor_scalar(dst[:].rearrange("p k n -> p (k n)"), ld, -1.0, None, ALU.max)\
                    .then_inc(quant, 1)
                n += 1
            dve.wait_ge(quant, n)
            nc.vector.memset(kst[:].rearrange("p c a b t -> p (c a b t)").bitcast(F32), 0.0).then_inc(quant, 1)
            dve.wait_ge(w_loaded, 16 * N_W)
            nc.vector.tensor_copy(lens_f[:], lens_i[:]).then_inc(quant, 1)
            dve.wait_ge(quant, n + 2)
            dve.wait_ge(consts_ready, 7)

            def statistics(it, s, b):
                n = s * IB + b
                c = b // CB
                if s == 0:
                    src = x_ld
                    dve.wait_ge(x_loaded, it * 16 + 16)
                else:
                    src = xr
                    if s == 2:
                        ffn_added.done(dve, it, c)
                    else:
                        att_added.done(dve, it, IB * (s // 2) + b)
                moments.slot(dve, it, n, IB)
                nc.vector.bn_stats(stats[:, b], src[:, b, :]).then_inc(stats_done.sem, 1)

            def aggregate(it, s, b):
                n = s * IB + b
                stats_done.done(dve, it, n)
                normed.slot(dve, it, n, IB)
                carry(dve, dve_tally)
                nc.vector.bn_aggr(mv[:, b], stats[:, b]).then_inc(moments.sem, 1)

            def normalise(it, s, c):
                rstd_ready.done(dve, it, s * NC + c)
                xT_ready.slot(dve, it, s * NC + c, NC)
                for b in range(CB):
                    src = (x_ld if s == 0 else xr)[:, c * CB + b, :]
                    k = c * CB + b
                    nc.vector.tensor_scalar(xn[c][:, b], src, mv[:, k, 0:1], rstd[:, k:k + 1], ALU.subtract,
                                            ALU.mult).then_inc(normed.sem, 1)

            def low_parts(it, l, c, j):
                src = S[0] if j else S[1]
                for m in range(KD):
                    qk_high.done(dve, it, part_index(l, c, j, m))
                    nc.vector.scalar_tensor_tensor(out=packed[:, c, j, 1, m], in0=src[:, m * CT:m * CT + CT],
                                                   scalar=bqk[:, l, j, m:m + 1], in1=packed[:, c, j, 0, m],
                                                   op0=ALU.add, op1=ALU.subtract).then_inc(qk_low.sem, 1)

            def values(it, l, c):
                v_ready.done(dve, it, 2 * l + c)
                mixed_ready.slot(dve, it, l * IB + c * CB + CB - 1, IB)
                for b in range(CB):
                    nc.vector.tensor_tensor(v2[:, c, b, :, 0:4:3, :],
                                            S[1][:, b * D:b * D + D].rearrange("p (a s d) -> p a s d", a=PAIRS, s=2),
                                            bvb[:, l].rearrange("p (a s d) -> p a s d", a=PAIRS, s=2),
                                            ALU.add).then_inc(v_copied.sem, 1)

            def attention(it, l):
                for t in range(UNITS + 9):
                    b1_, b2_, b3_ = t - 6, t - 8, t - 9
                    if t < UNITS:
                        g = UNITS * l + t
                        scores_ready.done(dve, it, g)
                        if g >= 4:
                            probsT_ready.done(dve, it, 2 * (g - 4) + 1)
                        elif g < 2:
                            ctxT_ready.done(dve, it, NC - 1)
                        else:
                            bias_added.done(dve, it, NC - 1)
                            normed.done(dve, it, IB - 1)
                        nc.vector.tensor_tensor(sm[:, g % 4], S[t % 2][:].rearrange("p (h t) -> p h t", t=P),
                                                bound[:, l, t // 2].unsqueeze(1).to_broadcast([P, UH, P]),
                                                ALU.min).then_inc(masked.sem, 1)
                    if b1_ >= 0 and b1_ % 2 == 0 and b1_ // 2 < IB:
                        g = l * IB + b1_ // 2
                        mixed_ready.done(dve, it, g)
                        attT_ready.slot(dve, it, g, 2)
                        nc.vector.reciprocal(rden[:, g % 2], V[:, 2 * P:4 * P]).then_inc(recip_done.sem, 1)
                    if 1 <= t <= UNITS:
                        g = UNITS * l + t - 1
                        masked.done(dve, it, g)
                        shifted.slot(dve, it, g, 4)
                        nc.vector.reduce_max(mx[:, g % 4], sm[:, g % 4], AX.X).then_inc(max_done.sem, 1)
                    if b1_ >= 0 and b1_ % 2 == 0 and b1_ // 2 < IB:
                        g = l * IB + b1_ // 2
                        recip_done.done(dve, it, g)
                        oproj_ready.slot(dve, it, g, 2)
                        nc.vector.tensor_tensor(attT[:, g % 2], V[:, 0:2 * P], rden[:, g % 2], ALU.mult)\
                            .then_inc(attT_ready.sem, 1)
                    if b2_ >= 0 and b2_ % 2 == 0 and b2_ // 2 < IB:
                        b = b2_ // 2
                        g = l * IB + b
                        oproj_ready.done(dve, it, g)
                        if l == 0:
                            bias_added.done(dve, it, b // CB)
                        nc.vector.tensor_tensor(xr[:, b], O[:, 0:D], xr[:, b], ALU.add).then_inc(att_added.sem, 1)
                    if b3_ >= 0 and b3_ % 2 == 0 and b3_ // 2 < IB:
                        statistics(it, 2 * l + 1, b3_ // 2)
                    if t - 10 >= 0 and t % 2 == 0 and (t - 10) // 2 < IB:
                        aggregate(it, 2 * l + 1, (t - 10) // 2)
                    if t == 19:
                        normalise(it, 2 * l + 1, 0)
                normalise(it, 2 * l + 1, 1)

            with dve.Fori(0, ITERS) as it:
                for b in range(IB):
                    statistics(it, 0, b)
                for b in range(IB):
                    aggregate(it, 0, b)
                scores_ready.past(dve, it, 2 * UNITS - 1)
                masked.past(dve, it, 2 * UNITS - 1)
                dve.wait_ge(mask_loaded, it * 16 + 16)
                nc.vector.tensor_scalar(bound[:, 0], mask_ld, 0.0, HUGE, ALU.not_equal, ALU.mult)\
                    .then_inc(bound_part.sem, 1)
                for b in range(IB):
                    ins = nc.vector.tensor_scalar(bound[:, 1, b], kpos[:], lens_f[:, bass.ds(it * IB + b, 1)], HUGE, ALU.is_lt,
                                                  ALU.mult)
                ins.then_inc(bound_part.sem, 1)
                bound_part.done(dve, it, 0)
                nc.vector.tensor_scalar(bound[:, 0], bound[:, 0], FILL[0], None, ALU.add)\
                    .then_inc(bound_ready.sem, 1)
                bound_part.done(dve, it, 1)
                nc.vector.tensor_scalar(bound[:, 1], bound[:, 1], FILL[1], None, ALU.add)\
                    .then_inc(bound_ready.sem, 1)
                for l in range(2):
                    for c in range(NC):
                        low_parts(it, l, c, 1)
                        values(it, l, c)
                        if c == 0:
                            for n in range(NC):
                                normalise(it, 2 * l, n)
                    for c in range(NC):
                        low_parts(it, l, c, 0)
                    attention(it, l)
                    if l == 0:
                        for c in range(NC):
                            xT_copied.done(dve, it, NC + c)
                            nc.vector.tensor_tensor(xs16[c][:, 1].rearrange("p k t -> p (k t)"), S[0][:],
                                                    xs16[c][:, 0].rearrange("p k t -> p (k t)"),
                                                    ALU.subtract).then_inc(x_low.sem, 1)
                            if c == 0:
                                scores_ready.done(dve, it, UNITS - 1)
                            else:
                                for k in range(NC):
                                    dve.wait_ge(stacked[k], (it * 2 + 1) * STACK + 16)
                            for j in range(KF // 2):
                                h_relu.done(dve, it, KF * c + 2 * j + 1)
                                nc.vector.tensor_copy(hh[c][:, 2 * j:2 * j + 2], work[:, j % 2])\
                                    .then_inc(h_high.sem, 1)
                                h_high.done(dve, it, 4 * c + j)
                                nc.vector.tensor_tensor(hl[c][:, 2 * j:2 * j + 2], work[:, j % 2],
                                                        hh[c][:, 2 * j:2 * j + 2], ALU.subtract)\
                                    .then_inc(h_low.sem, 1)
                        for c in range(NC):
                            ffn_ready.done(dve, it, c)
                            bias_added.done(dve, it, NC + c)
                            blk = xr[:, c * CB:c * CB + CB].rearrange("p b d -> p (b d)")
                            nc.vector.tensor_tensor(blk, S[1][:], blk, ALU.add).then_inc(ffn_added.sem, 1)
                            for b in range(CB):
                                statistics(it, 2, c * CB + b)
                            for b in range(CB):
                                aggregate(it, 2, c * CB + b)

                def choose(c):
                    loss_ready.done(dve, it, c)
                    k = c * CB * E
                    best_loss.past(dve, it, NC * CB - 1)
                    nc.vector.tensor_scalar(lneg[:, k:k + CB * E], V[0:1, 0:CB * E], -1.0, None, ALU.mult)\
                        .then_inc(loss_out.sem, 1)
                    loss_out.done(dve, it, c)
                    carry(dve, dve_tally)
                    for b in range(CB):
                        nc.vector.max(lmax[:, c * CB + b], lneg[:, k + b * E:k + b * E + E])\
                            .then_inc(best_loss.sem, 1)
                    for b in range(CB):
                        best_loss.done(dve, it, c * CB + b)
                        carry(dve, dve_tally)
                        nc.vector.max_index(lidx[:, c * CB + b], lmax[:, c * CB + b],
                                            lneg[:, k + b * E:k + b * E + E]).then_inc(expert_found.sem, 1)

                for c in range(NC):
                    xT_copied.done(dve, it, 3 * NC + c)
                    for e in range(E):
                        n = E * c + e
                        recon_ready.done(dve, it, n)
                        if n >= 2:
                            squared.done(dve, it, CB * (n - 1) - 1)
                        else:
                            h_low.done(dve, it, KF - 1)
                        for k in range(KD):
                            nc.vector.scalar_tensor_tensor(
                                out=work[:, e % 2, k], in0=S[(e + 1) % 2][:, k * CT:k * CT + CT],
                                scalar=bd2s[:, e, k:k + 1], in1=xT[c][:, k], op0=ALU.add,
                                op1=ALU.subtract).then_inc(diffed.sem, 1)
                        if c == 1 and e == 1:
                            choose(0)
                choose(1)
                for c in range(NC):
                    up_ready.done(dve, it, c)
                    blk = xr[:, c * CB:c * CB + CB].rearrange("p b d -> p (b d)")
                    nc.vector.tensor_tensor(blk, S[c][:], blk, ALU.add).then_inc(y_ready.sem, 1)

        @block.tensor
        def _(pe):
            for s in (ctxT_ready, xT_ready, q_ready, k_ready, v_ready, scores_ready, probsT_ready,
                      mixed_ready, oproj_ready, h_ready, ffn_ready, hd_ready, recon_ready, loss_ready,
                      down_ready, up_ready):
                s.prime(pe)
            pe.wait_ge(w_loaded, 16 * N_W)
            pe.wait_ge(consts_ready, 7)
            pe.wait_ge(quant, 13)

            reader = {"S0": (y_ready, 0), "S1": (y_ready, 1), "T0": (a_relu, CB - 1), "T1": (a_relu, 2 * CB - 1),
                      "V": (loss_out, 1), "O": (att_added, 2 * IB - 1)}
            first = dict(reader)
            seen = set()

            def claim(it, tile, signal_, n):
                sig, m = reader[tile]
                if tile in seen:
                    sig.done(pe, it, m)
                else:
                    sig.past(pe, it, m)
                seen.add(tile)
                reader[tile] = (signal_, n)

            def flip(it, dst, src, last):
                for k in range(KD):
                    for b in range(CB):
                        ins = nc.tensor.transpose(dst[:, k * CT + b * P:k * CT + b * P + P],
                                                  src[:, b, k * P:k * P + P], ident[:])
                ins.then_inc(last.sem, 1)

            def transpose_x(it, s, c):
                claim(it, "S0", *((x_low, c) if s == 1 else (xT_copied, s * NC + c)))
                normed.done(pe, it, s * IB + c * CB + CB - 1)
                flip(it, S[0], xn[c], xT_ready)

            def project(dst, w, src, last):
                for m in range(KD):
                    for k in range(KD):
                        ins = nc.tensor.matmul(dst[:, m * CT:m * CT + CT], w[:, k, m * P:m * P + P], src[:, k],
                                               start=(k == 0), stop=(k == KD - 1))
                ins.then_inc(last.sem, 1)

            def attention(it, l):
                def scores(u):
                    g = UNITS * l + u
                    b, c = u // 2, u // 8
                    claim(it, f"S{u % 2}", masked, g)
                    if u % 8 == 0:
                        pe.wait_ge(stacked[c], (it * 2 + l + 1) * STACK + 16)
                    t0 = (b % CB) * P
                    for a in range(4):
                        pair = 4 * (u % 2) + a
                        ins = nc.tensor.matmul(
                            S[u % 2][:, a * 2 * P:a * 2 * P + 2 * P], qst[:, c, pair, t0:t0 + P],
                            kst[:, c, pair, :, t0:t0 + P], start=True, stop=True)
                    ins.then_inc(scores_ready.sem, 1)

                def transposes(u):
                    g = UNITS * l + u
                    exp_done.done(pe, it, g)
                    for q in range(2):
                        claim(it, f"T{q}", probsT_copied, 2 * g + q)
                        for h in range(4):
                            ins = nc.tensor.transpose(T[q][:, h * P:h * P + P], sm[:, g % 4, 4 * q + h], ident[:])
                        ins.then_inc(probsT_ready.sem, 1)

                def mix(u):
                    g = UNITS * l + u
                    b, half = u // 2, u % 2
                    c = b // CB
                    if half == 0:
                        claim(it, "V", attT_ready, l * IB + b)
                        v_copied.done(pe, it, l * IB + b)
                    probsT_copied.done(pe, it, 2 * g + 1)
                    for part in range(2):
                        for s in range(2):
                            for a in range(4):
                                pair = 4 * half + a
                                w = v2[:, c, b % CB, pair, 2 * s:2 * s + 2] if part == 0 else sel[:, s]
                                if part == 0:
                                    w = w.rearrange("p s d -> p (s d)")
                                ins = nc.tensor.matmul(
                                    V[32 * a:32 * a + 32, (2 * part + half) * P:(2 * part + half) * P + P], w,
                                    pT[:, half, 2 * a + s], start=(s == 0), stop=(s == 1))
                    if half:
                        ins.then_inc(mixed_ready.sem, 1)

                def output(b):
                    g = l * IB + b
                    claim(it, "O", att_added, g)
                    attT_ready.done(pe, it, g)
                    for k in range(KD):
                        ins = nc.tensor.matmul(O[:, 0:D], attT[:, g % 2, k * P:k * P + P], wo[l][:, k],
                                               start=(k == 0), stop=(k == KD - 1))
                    ins.then_inc(oproj_ready.sem, 1)

                for t in range(UNITS + LAG + 4):
                    if t < UNITS:
                        scores(t)
                    if LAG <= t < UNITS + LAG:
                        transposes(t - LAG)
                    if LAG + 1 <= t < UNITS + LAG + 1:
                        mix(t - LAG - 1)
                    if t >= 7 and t % 2 == 1 and (t - 7) // 2 < IB:
                        output((t - 7) // 2)

            with pe.Fori(0, ITERS) as it:
                pe.wait_ge(ctx_loaded, it * 16 + 16)
                for c in range(NC):
                    claim(it, f"S{c}", ctxT_copied, c)
                    flip(it, S[c], ctx_ld[:, c * CB:c * CB + CB], ctxT_ready)
                for l in range(2):
                    for c in range(NC):
                        if l == 0:
                            ctxT_copied.done(pe, it, c)
                        claim(it, "S0", qk_low, part_index(l, c, 1, KD - 1))
                        project(S[0], wk[l], ctxT[:, c], k_ready)
                        claim(it, "S1", v_copied, l * IB + c * CB + CB - 1)
                        for b in range(CB):
                            for k in range(KD):
                                ins = nc.tensor.matmul(S[1][:, b * D:b * D + D], ctxT[:, c, k, b * P:b * P + P],
                                                       wv[l][:, k], start=(k == 0), stop=(k == KD - 1))
                        ins.then_inc(v_ready.sem, 1)
                    for c in range(NC):
                        transpose_x(it, 2 * l, c)
                        claim(it, "S1", qk_low, part_index(l, c, 0, KD - 1))
                        xT_copied.done(pe, it, 2 * l * NC + c)
                        project(S[1], wq[l], xT[c], q_ready)
                    attention(it, l)
                    if l == 0:
                        for c in range(NC):
                            transpose_x(it, 1, c)
                            x_low.done(pe, it, c)
                            for j in range(KF // 2):
                                claim(it, f"S{(j + 1) % 2}", h_relu, KF * c + 2 * j + 1)
                                for m in range(2):
                                    f0 = (2 * j + m) * P
                                    for n in range(2 * KD):
                                        k, part = n // 2, n % 2
                                        ins = nc.tensor.matmul(S[(j + 1) % 2][:, m * CT:m * CT + CT],
                                                               w1q[:, k, f0:f0 + P], xs16[c][:, part, k],
                                                               start=(n == 0), stop=(n == 2 * KD - 1))
                                ins.then_inc(h_ready.sem, 1)
                        for c in range(NC):
                            claim(it, "S1", ffn_added, c)
                            h_low.done(pe, it, 4 * c + 3)
                            for b in range(CB):
                                for n in range(2 * KF):
                                    k, part = n // 2, (hh, hl)[n % 2][c]
                                    ins = nc.tensor.matmul(S[1][:, b * D:b * D + D], part[:, k, b * P:b * P + P],
                                                           w2q[:, k], start=(n == 0), stop=(n == 2 * KF - 1))
                            ins.then_inc(ffn_ready.sem, 1)
                for c in range(NC):
                    transpose_x(it, 3, c)
                    xT_copied.done(pe, it, 3 * NC + c)
                    for j in range(2):
                        claim(it, f"S{(j + 1) % 2}", hd_relu, 4 * c + 2 * j + 1)
                        for m in range(2):
                            e0 = 2 * (2 * j + m)
                            for k in range(KD):
                                ins = nc.tensor.matmul(S[(j + 1) % 2][:, m * CT:m * CT + CT],
                                                       wd1s[:, k, e0:e0 + 2].rearrange("p e r -> p (e r)"),
                                                       xT[c][:, k], start=(k == 0), stop=(k == KD - 1))
                        ins.then_inc(hd_ready.sem, 1)
                    for e in range(E):
                        claim(it, f"S{(e + 1) % 2}", diffed, (E * c + e) * KD + 1)
                        hd_relu.done(pe, it, 4 * c + e // 2)
                        for m in range(KD):
                            ins = nc.tensor.matmul(S[(e + 1) % 2][:, m * CT:m * CT + CT],
                                                   wd2s[:, e, m * P:m * P + P], hd[c][:, e // 2],
                                                   start=True, stop=True)
                        ins.then_inc(recon_ready.sem, 1)
                    claim(it, "V", loss_out, c)
                    squared.done(pe, it, CB * E * (c + 1) - 1)
                    nc.tensor.matmul(V[0:1, 0:CB * E], ones[:], acc[:, CB * E * c:CB * E * c + CB * E],
                                     start=True, stop=True).then_inc(loss_ready.sem, 1)
                for c in range(NC):
                    pe.wait_ge(gathered, (it * NC + c + 1) * GATHER)
                    claim(it, f"T{c}", a_relu, c * CB + CB - 1)
                    for b in range(CB):
                        for k in range(KD):
                            ins = nc.tensor.matmul(T[c][0:R, b * P:b * P + P], dws[:, b, k], xT[c][:, k, b * P:b * P + P],
                                                   start=(k == 0), stop=(k == KD - 1))
                    ins.then_inc(down_ready.sem, 1)
                    claim(it, f"S{c}", y_ready, c)
                    for b in range(CB):
                        for k in range(KD):
                            nc.tensor.matmul(S[c][:, b * D:b * D + D], xT[c][:, k, b * P:b * P + P], wb[:, k],
                                             start=(k == 0), stop=False)
                        a_relu.done(pe, it, c * CB + b)
                        ins = nc.tensor.matmul(S[c][:, b * D:b * D + D], aT[:, b * P:b * P + P], ups[:, b],
                                               start=False, stop=True)
                    ins.then_inc(up_ready.sem, 1)
            assert reader == first, reader


_ARGS = [
    ("x", "x"), ("ctx", "ctx_1024"), ("lens", "_lenS2"), ("mask", "mask_Bx1xSxS2_if1"),
    ("wq0", "L0_xattn_w_q"), ("bq0", "L0_xattn_b_q"), ("wk0", "L0_xattn_w_k"), ("bk0", "L0_xattn_b_k"),
    ("wv0", "L0_xattn_w_v"), ("bv0", "L0_xattn_b_v"), ("wo0", "L0_xattn_w_o"), ("bo0", "L0_xattn_b_o"),
    ("w1t", "L0_ffn_W1"), ("b1", "L0_ffn_b1"), ("w2t", "L0_ffn_W2"), ("b2", "L0_ffn_b2"),
    ("wq1", "L1_xattn_W_q"), ("wk1", "L1_xattn_W_k"), ("wv1", "L1_xattn_W_v"), ("wo1", "L1_xattn_W_o"),
    ("w_base", "L1_ffn_W_base"), ("b_base", "L1_ffn_b_base"), ("wd1", "L1_ffn_Wd1"), ("bd1", "L1_ffn_bd1"),
    ("wd2", "L1_ffn_Wd2"), ("bd2", "L1_ffn_bd2"), ("wa_down", "L1_ffn_Wa_down"), ("ba_down", "L1_ffn_ba_down"),
    ("wa_up", "L1_ffn_Wa_up"), ("ba_up", "L1_ffn_ba_up"),
]
_TRANSPOSED = {"w1t", "w2t", "wq1", "wk1", "wv1", "wo1"}


def kernel(**inputs):
    import concourse.bacc as bacc
    from concourse.bass_utils import run_bass_kernel_spmd

    nc = bacc.Bacc("TRN2", target_bir_lowering=False, num_devices=1)
    arrays, args = {}, []
    for name, key in _ARGS:
        a = np.asarray(inputs[key])
        a = np.ascontiguousarray(a.T if name in _TRANSPOSED else a)
        arrays[f"in_{name}"] = a
        args.append(nc.dram_tensor(f"in_{name}", a.shape, mybir.dt.from_np(a.dtype), kind="ExternalInput").ap())
    y = nc.dram_tensor("out_y", (B, P, D), F32, kind="ExternalOutput").ap()
    nc.disable_value_cache = True
    build(nc, *args, y)
    r = run_bass_kernel_spmd(nc, [arrays], core_ids=[0])
    return r.results[0]["out_y"]
```

```python
from contextlib import ExitStack

import numpy as np

import concourse.bass as bass
from concourse import mybir

F32 = mybir.dt.float32
F16 = mybir.dt.float16
BF16 = mybir.dt.bfloat16
I32 = mybir.dt.int32
U32 = mybir.dt.uint32
ALU = mybir.AluOpType
ACT = mybir.ActivationFunctionType
AX = mybir.AxisListType
RADD = bass.bass_isa.ReduceOp.add

P = 128
B = 64
D = 256
KD = D // P
H = 16
HD = D // H
F = 1024
KF = F // P
E = 8
R = 64
CB = 4
NC = 2
IB = CB * NC
ITERS = B // IB
CT = CB * P
AW = KD * R + D + 1
UNITS = 2 * IB
UH = H // 2
PAIRS = H // 2
EARLY_K = (10, 14)
LAG = 3
EPS = 1e-5
HUGE = 3e38
ROUND = 1.5 * 2.0 ** 23
SCALE = 0.25
FILL = (-4e9, -4e6)


def carry(eng, tally):
    eng.sem_inc(tally, 1)


def part_index(l, c, j, m):
    return ((2 * l + 1 - j) * NC + c) * KD + m


class Signal:

    def __init__(self, sem, per):
        self.sem, self.per = sem, per

    def prime(self, eng):
        eng.sem_inc(self.sem, self.per)

    def done(self, eng, it, n):
        if isinstance(it, int) and it * self.per + n + 1 <= 0:
            return
        eng.wait_ge(self.sem, it * self.per + (self.per + n + 1))

    def past(self, eng, it, n):
        self.done(eng, it, n - self.per)

    def slot(self, eng, it, n, slots):
        if n >= slots:
            self.done(eng, it, n - slots)
        else:
            self.past(eng, it, self.per + n - slots)


def build(nc, x, ctx_in, lens, mask, wq0, bq0, wk0, bk0, wv0, bv0, wo0, bo0, w1t, b1, w2t, b2,
          wq1, wk1, wv1, wo1, w_base, wd1, bd1, wd2, bd2, adapters, out):
    with ExitStack() as ctx:
        def sb(name, shape, dt):
            return ctx.enter_context(nc.sbuf_tensor(name, shape, dt))

        def pb(name, shape):
            return ctx.enter_context(nc.psum_tensor(name, shape, F32))

        def sem(name):
            return ctx.enter_context(nc.semaphore(name))

        wq = [sb(f"wq{l}", [P, KD, D], F32) for l in range(2)]
        wk = [sb(f"wk{l}", [P, KD, D], F32) for l in range(2)]
        wv = [sb(f"wv{l}", [P, KD, D], F32) for l in range(2)]
        wo = [sb(f"wo{l}", [P, KD, D], F32) for l in range(2)]
        w1q = sb("w1q", [P, KD, F], F16)
        w2q = sb("w2q", [P, KF, D], F16)
        wb = sb("wb", [P, KD, D], F32)
        wd1s = sb("wd1s", [P, KD, E, R], F32)
        wd2s = sb("wd2s", [P, E, D], F32)
        bqk = sb("bqk", [P, 2, 2, KD], F32)
        bvb = sb("bvb", [P, 2, D], F32)
        bob = sb("bob", [P, D], F32)
        b2b = sb("b2b", [P, D], F32)
        b1s = sb("b1s", [P, KF], F32)
        bd1s = sb("bd1s", [P, E // 2], F32)
        bd2s = sb("bd2s", [P, E, KD], F32)
        ident = sb("ident", [P, P], F32)
        sel = sb("sel", [P, 2, 2 * HD], F32)
        ones = sb("ones", [P, 1], F32)
        kpos = sb("kpos", [P, P], F32)
        mhalf = sb("mhalf", [P, CB], F32)
        lens_i = sb("lens_i", [P, B], I32)
        lens_f = sb("lens_f", [P, B], F32)
        gam = sb("gam", [P, 8], F32)

        xr = sb("xr", [P, IB, D], F32)
        ctxT = sb("ctxT", [P, NC, KD, CT], F32)
        bound = sb("bound", [P, 2, IB, P], BF16)
        xn = [sb(f"xn{c}", [P, CB, D], F32) for c in range(NC)]
        xT = [sb(f"xT{c}", [P, KD, CT], F32) for c in range(NC)]
        stats = sb("stats", [P, IB, 6], F32)
        mv = sb("mv", [P, IB, 2], F32)
        veps = sb("veps", [P, IB], F32)
        rstd = sb("rstd", [P, IB], F32)
        packed = sb("packed", [P, NC, 2, 2, KD, CT], F16)
        qst = sb("qst", [P, NC, 4, KD, CT], F16)
        kst = sb("kst", [P, NC, 4, 2, KD, CT], F16)
        v2 = sb("v2", [P, NC, CB, PAIRS, 4, HD], F32)
        sm = sb("sm", [P, 4, UH, P], F32)
        mx = sb("mx", [P, 4, UH], F32)
        pT = sb("pT", [P, 2, UH, P], F32)
        mixed = sb("mixed", [P, 2, 4 * P], F32)
        attT = mixed[:, :, 0:2 * P]
        work = sb("work", [P, 2, 2, CT], F32)
        acc = sb("acc", [P, NC * CB * E], F32)
        lneg = sb("lneg", [1, NC * CB * E], F32)
        lmax = sb("lmax", [1, NC * CB, 8], F32)
        lidx = sb("lidx", [1, NC * CB, 8], U32)
        adapter0 = sb("adapter0", [P, CB, AW], F32)
        aT = sb("aT", [R + 2, CT], F32)

        pT1 = pT[:, 1].rearrange("p h t -> p (h t)")
        mixed_all = mixed[:].rearrange("p s t -> p (s t)")
        adapter = [[adapter0[:, b] for b in range(CB)],
                   [pT1[:, 0:AW], pT1[:, AW:2 * AW], mixed_all[:, 0:AW], mixed_all[:, AW:2 * AW]]]
        ctx_ld = sm[:, 0:2].rearrange("p s h t -> p (s h t)").rearrange("p (b d) -> p b d", d=D)
        x_ld = sm[:, 2:4].rearrange("p s h t -> p (s h t)").rearrange("p (b d) -> p b d", d=D)
        mask_ld = pT[:, 0].rearrange("p h t -> p (h t)").rearrange("p (b t) -> p b t", t=P).bitcast(I32)
        xs16 = [xT[c][:].rearrange("p k t -> p (k t)").bitcast(F16)
                .rearrange("p (s k t) -> p s k t", s=2, k=KD) for c in range(NC)]
        hh = [qst[:, 0].rearrange("p r k t -> p (r k) t"), packed[:, 0].rearrange("p a b k t -> p (a b k) t")]
        hl = [qst[:, 1].rearrange("p r k t -> p (r k) t"), packed[:, 1].rearrange("p a b k t -> p (a b k) t")]
        hd = [qst[:, c].rearrange("p r k t -> p (r k t)").bitcast(F32)
              .rearrange("p (m t) -> p m t", m=E // 2) for c in range(NC)]
        w1_ld = kst[:, 0].rearrange("p r s k t -> p (r s k t)").bitcast(F32)[:, 0:KD * F]
        w2_ld = kst[:, 1].rearrange("p r s k t -> p (r s k t)").bitcast(F32)[:, 0:KF * D]

        S = [pb(f"psS{k}", [P, 1024]) for k in range(2)]
        T = [pb(f"psT{k}", [P, 512]) for k in range(2)]
        V = pb("psV", [P, 512])
        O = pb("psO", [P, 512])

        def signal(name, per):
            return Signal(sem(name), per)

        ctxT_ready = signal("ctxT_ready", NC)
        xT_ready = signal("xT_ready", 4 * NC)
        q_ready = signal("q_ready", 2 * NC)
        k_ready = signal("k_ready", 2 * NC)
        v_ready = signal("v_ready", 2 * NC)
        scores_ready = signal("scores_ready", 2 * UNITS)
        probsT_ready = signal("probsT_ready", 4 * UNITS)
        mixed_ready = signal("mixed_ready", 2 * IB)
        oproj_ready = signal("oproj_ready", 2 * IB)
        h_ready = signal("h_ready", KF)
        ffn_ready = signal("ffn_ready", NC)
        hd_ready = signal("hd_ready", 2 * NC)
        recon_ready = signal("recon_ready", NC * E)
        loss_ready = signal("loss_ready", NC)
        down_ready = signal("down_ready", NC)
        up_ready = signal("up_ready", NC)
        ctxT_copied = signal("ctxT_copied", NC)
        xT_copied = signal("xT_copied", 4 * NC)
        qk_high = signal("qk_high", 2 * NC * 2 * KD)
        exp_done = signal("exp_done", 2 * UNITS)
        probsT_copied = signal("probsT_copied", 4 * UNITS)
        mixed_copied = signal("mixed_copied", 2 * IB)
        h_relu = signal("h_relu", NC * KF)
        hd_relu = signal("hd_relu", NC * E // 2)
        squared = signal("squared", NC * E * CB)
        a_relu = signal("a_relu", NC * CB)
        bound_part = signal("bound_part", 2)
        bound_ready = signal("bound_ready", 2)
        stats_done = signal("stats_done", 4 * IB)
        moments = signal("moments", 4 * IB)
        normed = signal("normed", 4 * IB)
        qk_low = signal("qk_low", 2 * NC * 2 * KD)
        v_copied = signal("v_copied", 2 * IB)
        masked = signal("masked", 2 * UNITS)
        max_done = signal("max_done", 2 * UNITS)
        recip_done = signal("recip_done", 2 * IB)
        attT_ready = signal("attT_ready", 2 * IB)
        att_added = signal("att_added", 2 * IB)
        x_low = signal("x_low", NC)
        h_high = signal("h_high", KF)
        h_low = signal("h_low", KF)
        ffn_added = signal("ffn_added", NC)
        diffed = signal("diffed", NC * E * KD)
        loss_out = signal("loss_out", NC)
        best_loss = signal("best_loss", NC * CB)
        expert_found = signal("expert_found", NC * CB)
        y_ready = signal("y_ready", NC)
        veps_ready = signal("veps_ready", 4 * NC)
        rstd_ready = signal("rstd_ready", 4 * NC)
        bias_added = signal("bias_added", 2 * NC)
        shifted = signal("shifted", 2 * UNITS)
        STACK_K = 16 * 2 * 4 * 4
        STACK = STACK_K + 16 * 4 * 4
        GATHER = 16 * CB
        x_loaded, ctx_loaded, mask_loaded = sem("x_loaded"), sem("ctx_loaded"), sem("mask_loaded")
        stacked = [sem(f"stacked{c}") for c in range(NC)]
        gathered = [sem(f"gathered{c}") for c in range(NC)]
        stored = [sem(f"stored{c}") for c in range(NC)]
        w_loaded, ffn_w_loaded = sem("w_loaded"), sem("ffn_w_loaded")
        wd2_loaded = sem("wd2_loaded")
        consts_set, consts_ready = sem("consts_set"), sem("consts_ready")
        zeros_set, gamma_part, gamma_sum = sem("zeros_set"), sem("gamma_part"), sem("gamma_sum")
        quant, staged_free = sem("quant"), sem("staged_free")

        dve_tally, pool_tally, sp_tally = sem("dve_tally"), sem("pool_tally"), sem("sp_tally")

        xv = x.rearrange("b s d -> s b d")
        cv = ctx_in.rearrange("b s d -> s b d")
        mv_dram = mask.rearrange("b o q k -> q (b o) k")
        outv = out.rearrange("b s d -> s b d")

        def rows(w):
            return w.rearrange("(k p) n -> p k n", p=P)

        def col(b):
            return b.rearrange("(k p) -> p k", p=P)

        def everywhere(b):
            return b.rearrange("(a n) -> a n", a=1).to_broadcast([P, D])

        WEIGHTS = [(ctx_w[:], rows(src)) for ctx_w, src in (
            (wk[0], wk0), (wv[0], wv0), (wq[0], wq0), (wo[0], wo0), (wk[1], wk1), (wv[1], wv1),
            (wq[1], wq1), (wo[1], wo1), (wb, w_base))]
        WEIGHTS += [(bqk[:, 0, 0, :], col(bq0)), (bqk[:, 0, 1, :], col(bk0)),
                    (bvb[:, 0, :], everywhere(bv0)), (bob[:], everywhere(bo0)), (b2b[:], everywhere(b2)),
                    (b1s[:], col(b1)),
                    (bd1s[:], bd1.rearrange("(m e) r -> (e r) m", e=2)),
                    (lens_i[:], lens.rearrange("(a n) -> a n", a=1).to_broadcast([P, B]))]
        WEIGHTS += [(wd1s[:, k], wd1[:, P * k:P * k + P, :].rearrange("e p r -> p e r")) for k in range(KD)]
        WEIGHTS += [(bd2s[:, :, k], bd2[:, P * k:P * k + P].rearrange("e p -> p e")) for k in range(KD)]
        WEIGHTS += [(wd2s[R * s:R * s + R, s:E:2, :], wd2[s:E:2].rearrange("e r d -> r e d")) for s in range(2)]
        N_W = len(WEIGHTS)

        N_ZEROS = 3

        block = ctx.enter_context(nc.Block())

        @block.sync
        def _(sp):
            n_ffn = 0
            for dst, src in ((w1_ld.rearrange("p (k f) -> p k f", k=KD), w1t.rearrange("(k p) f -> p k f", p=P)),
                             (w2_ld.rearrange("p (k d) -> p k d", k=KF), w2t.rearrange("(k p) d -> p k d", p=P))):
                sp.dma_start(dst, src).then_inc(ffn_w_loaded, 16)
                n_ffn += 1
            sp.wait_ge(zeros_set, N_ZEROS)
            with nc.allow_non_contiguous_dma(reason="biases, one or a few for each partition, once"):
                for dst, src in WEIGHTS:
                    sp.dma_start(dst, src).then_inc(w_loaded, 16)

            def load(b0):
                sp.dma_start(ctx_ld, cv[:, bass.ds(b0, IB), :]).then_inc(ctx_loaded, 16)
                sp.dma_start(x_ld, xv[:, bass.ds(b0, IB), :]).then_inc(x_loaded, 16)
                sp.dma_start(mask_ld, mv_dram[:, bass.ds(b0, IB), :]).then_inc(mask_loaded, 16)

            def stack(it, l, c, j):
                scores_ready.done(sp, it, UNITS * (l - 1) + 8 * c + 7)
                if j == 0:
                    if l:
                        ffn_ready.done(sp, it, 0)
                    else:
                        recon_ready.past(sp, it, NC * E - 1)
                qk_high.done(sp, it, part_index(l, c, j, KD - 1))
                qk_low.done(sp, it, part_index(l, c, j, KD - 1))
                for quad in range(4):
                    part = quad // 2 if j == 0 else quad % 2
                    src = packed[:, c, j, part].rearrange("p k t -> p (k t)")
                    for r in range(4):
                        if j == 0:
                            sp.dma_start(qst[32 * quad:32 * quad + 32, c, r].rearrange("p k t -> p (k t)"),
                                         src[32 * r:32 * r + 32]).then_inc(stacked[c], 16)
                        else:
                            for s in range(2):
                                row = 32 * quad + HD * s
                                sp.dma_start(kst[row:row + HD, c, r, s].rearrange("p k t -> p (k t)"),
                                             src[32 * r + HD * s:32 * r + HD * s + HD])\
                                    .then_inc(stacked[c], 16)

            load(0)
            stack(-1, 2, 0, 1)
            with sp.Fori(0, ITERS) as it:
                stack(it, 0, 0, 0)
                stack(it, 0, 1, 1)
                stack(it, 0, 1, 0)
                for c in range(NC):
                    stack(it, 1, c, 1)
                for c in range(NC):
                    stack(it, 1, c, 0)
                mixed_ready.done(sp, it, 2 * IB - 1)
                load((it + 1) % ITERS * IB)
                oproj_ready.done(sp, it, 2 * IB - 1)
                up_ready.past(sp, it, NC - 1)
                for c in range(NC):
                    for b in range(CB):
                        expert_found.done(sp, it, c * CB + b)
                        carry(sp, sp_tally)
                        e = sp.value_load(lidx[0:1, c * CB + b, 0:1], min_val=0, max_val=E - 1)
                        sp.dma_start(adapter[c][b], adapters[bass.ds(e, 1)].rearrange("a p n -> p (a n)"))\
                            .then_inc(gathered[c], 16)
                stack(it, 2, 0, 1)
            sp.wait_ge(stacked[0], ITERS * 2 * STACK + (STACK_K + 16))
            for loaded in (ctx_loaded, x_loaded, mask_loaded):
                sp.wait_ge(loaded, 16 * (ITERS + 1))
            sp.wait_ge(stored[0], 16 * (ITERS + 1))
            sp.wait_ge(stored[1], 16 * (ITERS + 1))

        @block.gpsimd
        def _(pool):
            for s in (veps_ready, rstd_ready, bias_added, shifted):
                s.prime(pool)
            nc.gpsimd.memset(ident[:], 0.0).then_inc(consts_set, 1)
            nc.gpsimd.memset(sel[:], 0.0).then_inc(consts_set, 1)
            nc.gpsimd.memset(ones[:], 1.0).then_inc(consts_ready, 1)
            nc.gpsimd.memset(mhalf[:], -0.5).then_inc(consts_ready, 1)
            nc.gpsimd.iota(kpos[:], pattern=[[1, P]], base=0, channel_multiplier=0,
                           allow_small_or_imprecise_dtypes=True).then_inc(consts_ready, 1)
            pool.wait_ge(consts_set, 2)
            nc.gpsimd.affine_select(out=ident[:], in_=ident[:], compare_op=ALU.not_equal, fill=1.0,
                                    base=0, pattern=[[-1, P]], channel_multiplier=1).then_inc(consts_ready, 1)
            nc.gpsimd.memset(sel[:, 0, 0:HD], 1.0).then_inc(consts_ready, 1)
            nc.gpsimd.memset(sel[:, 1, HD:2 * HD], 1.0).then_inc(consts_ready, 1)
            for w in range(2):
                pool.wait_ge(gamma_part, w + 1)
                nc.gpsimd.partition_all_reduce(gam[:, 2 + w:3 + w], gam[:, w:w + 1], P, RADD).then_inc(gamma_sum, 1)
            pool.wait_ge(w_loaded, 16 * N_W)
            pool.wait_ge(consts_ready, 7)

            def rstd_of(it, s, c):
                moments.done(pool, it, (s * NC + c) * CB + CB - 1)
                if s:
                    normed.done(pool, it, ((s - 1) * NC + c) * CB + CB - 1)
                else:
                    normed.past(pool, it, (3 * NC + c) * CB + CB - 1)
                b0 = c * CB
                carry(pool, pool_tally)
                nc.gpsimd.tensor_scalar(veps[:, b0:b0 + CB], mv[:, b0:b0 + CB, 1], EPS, None, ALU.add)\
                    .then_inc(veps_ready.sem, 1)
                veps_ready.done(pool, it, s * NC + c)
                nc.gpsimd.tensor_tensor(rstd[:, b0:b0 + CB], veps[:, b0:b0 + CB], mhalf[:, 0:CB], ALU.pow)\
                    .then_inc(rstd_ready.sem, 1)

            for c in range(NC):
                rstd_of(-1, 4, c)
            with pool.Fori(0, ITERS) as it:
                pool.wait_ge(x_loaded, it * 16 + 16)
                for c in range(NC):
                    pool.wait_ge(stored[c], it * 16 + 16)
                    nc.gpsimd.tensor_tensor(xr[:, c * CB:c * CB + CB, :], x_ld[:, c * CB:c * CB + CB, :],
                                            bob[:].unsqueeze(1).to_broadcast([P, CB, D]), ALU.add)\
                        .then_inc(bias_added.sem, 1)
                for l in range(2):
                    for u in range(UNITS):
                        g = UNITS * l + u
                        max_done.done(pool, it, g)
                        nc.gpsimd.tensor_tensor(sm[:, g % 4], sm[:, g % 4],
                                                mx[:, g % 4].unsqueeze(2).to_broadcast([P, UH, P]),
                                                ALU.subtract).then_inc(shifted.sem, 1)
                    for c in range(NC):
                        rstd_of(it, 2 * l + 1, c)
                    if l == 0:
                        for c in range(NC):
                            normed.done(pool, it, (NC + c) * CB + CB - 1)
                            blk = xr[:, c * CB:c * CB + CB, :]
                            nc.gpsimd.tensor_tensor(blk, blk, b2b[:].unsqueeze(1).to_broadcast([P, CB, D]),
                                                    ALU.add).then_inc(bias_added.sem, 1)
                        for c in range(NC):
                            rstd_of(it, 2, c)
                for c in range(NC):
                    rstd_of(it, 4, c)

        @block.scalar
        def _(act):
            for s in (ctxT_copied, xT_copied, qk_high, exp_done, probsT_copied, mixed_copied, h_relu, hd_relu,
                      squared, a_relu):
                s.prime(act)
            for c in range(NC):
                act.sem_inc(stored[c], 16)
                act.sem_inc(stacked[c], 16)
            act.wait_ge(w_loaded, 16 * N_W)

            def store(it, c):
                y_ready.done(act, it, c)
                act.dma_start(outv[:, bass.ds(it * IB + c * CB, CB), :],
                              xr[:, c * CB:c * CB + CB, :]).then_inc(stored[c], 16)

            def copy_xT(it, s, c):
                xT_ready.done(act, it, s * NC + c)
                if s == 0:
                    up_ready.past(act, it, c)
                elif s == 1:
                    q_ready.done(act, it, c)
                elif s == 2:
                    h_ready.done(act, it, 4 * c + 3)
                else:
                    q_ready.done(act, it, NC + c)
                if s == 1:
                    nc.scalar.activation(xs16[c][:, 0].rearrange("p k t -> p (k t)"), S[0][:], ACT.Copy)\
                        .then_inc(xT_copied.sem, 1)
                else:
                    nc.scalar.activation(xT[c][:].rearrange("p k t -> p (k t)"), S[0][:], ACT.Copy)\
                        .then_inc(xT_copied.sem, 1)

            def high_parts(it, l, c, j):
                (k_ready if j else q_ready).done(act, it, 2 * l + c)
                if j:
                    act.wait_ge(stacked[c], (it * 2 + l) * STACK + 16)
                elif l:
                    ffn_ready.done(act, it, 1)
                src = S[0] if j else S[1]
                for m in range(KD):
                    nc.scalar.activation(packed[:, c, j, 0, m], src[:, m * CT:m * CT + CT], ACT.Identity,
                                         bias=bqk[:, l % 2, j, m:m + 1]).then_inc(qk_high.sem, 1)

            def attention(it, l):
                for t in range(UNITS + 2 + LAG):
                    if l == 0 and t in EARLY_K:
                        high_parts(it, 1, EARLY_K.index(t), 1)
                    if t >= 6 and t % 2 == 0 and (t - 6) // 2 < IB:
                        g = l * IB + (t - 6) // 2
                        mixed_ready.done(act, it, g)
                        oproj_ready.slot(act, it, g, 2)
                        nc.scalar.activation(mixed[:, g % 2], V[:], ACT.Copy).then_inc(mixed_copied.sem, 1)
                    if 2 <= t < UNITS + 2:
                        g = UNITS * l + t - 2
                        shifted.done(act, it, g)
                        nc.scalar.activation(sm[:, g % 4], sm[:, g % 4], ACT.Exp, scale=SCALE)\
                            .then_inc(exp_done.sem, 1)
                    if LAG <= t < UNITS + LAG:
                        u = t - LAG
                        g = UNITS * l + u
                        if g >= 2:
                            mixed_ready.done(act, it, g // 2 - 1)
                        else:
                            mixed_ready.past(act, it, 2 * IB - 1)
                            bound_ready.done(act, it, 0)
                        for q in range(2):
                            probsT_ready.done(act, it, 2 * g + q)
                            nc.scalar.activation(pT[:, u % 2, 4 * q:4 * q + 4].rearrange("p h t -> p (h t)"),
                                                 T[q][:], ACT.Copy).then_inc(probsT_copied.sem, 1)

            def next_keys(it):
                for c in range(NC):
                    ctxT_ready.done(act, it, NC + c)
                    v_ready.done(act, it, 2 * NC - 1)
                    nc.scalar.activation(ctxT[:, c].rearrange("p k t -> p (k t)"), S[c][:], ACT.Copy)\
                        .then_inc(ctxT_copied.sem, 1)
                for c in range(NC):
                    high_parts(it, 2, c, 1)

            next_keys(-1)
            with act.Fori(0, ITERS) as it:
                for l in range(2):
                    for c in range(NC):
                        copy_xT(it, 2 * l, c)
                        high_parts(it, l, c, 0)
                    attention(it, l)
                    if l == 0:
                        for c in range(NC):
                            copy_xT(it, 1, c)
                            for m in range(KF):
                                if m % 2 == 0:
                                    h_ready.done(act, it, (KF * c + m) // 2)
                                    if KF * c + m >= 4:
                                        h_low.done(act, it, (KF * c + m) // 2 - 2)
                                    else:
                                        squared.past(act, it, squared.per - 1)
                                nc.scalar.activation(work[:, m // 2 % 2, m % 2],
                                                     S[(m // 2 + 1) % 2][:, (m % 2) * CT:(m % 2) * CT + CT],
                                                     ACT.Relu, bias=b1s[:, m:m + 1]).then_inc(h_relu.sem, 1)
                for c in range(NC):
                    copy_xT(it, 3, c)
                    scores_ready.done(act, it, 2 * UNITS - 1)
                    for m in range(E // 2):
                        if m % 2 == 0:
                            hd_ready.done(act, it, 2 * c + m // 2)
                        nc.scalar.activation(hd[c][:, m], S[(m // 2 + 1) % 2][:, (m % 2) * CT:(m % 2) * CT + CT],
                                             ACT.Relu, bias=bd1s[:, m:m + 1]).then_inc(hd_relu.sem, 1)
                    if c == 0:
                        loss_ready.past(act, it, NC - 1)
                    for e in range(E):
                        diffed.done(act, it, (E * c + e) * KD + 1)
                        for b in range(CB):
                            blk = work[:, e % 2, :, P * b:P * b + P]
                            k = (c * CB + b) * E + e
                            nc.scalar.activation(blk, blk, ACT.Square, accum_out=acc[:, k:k + 1])\
                                .then_inc(squared.sem, 1)
                next_keys(it)
                for c in range(NC):
                    down_ready.done(act, it, c)
                    if c:
                        up_ready.done(act, it, c - 1)
                    else:
                        up_ready.past(act, it, NC - 1)
                    for b in range(CB):
                        nc.scalar.activation(aT[0:R, P * b:P * b + P], T[c][0:R, P * b:P * b + P], ACT.Relu,
                                             bias=adapter[c][b][0:R, AW - 1:AW]).then_inc(a_relu.sem, 1)
                for c in range(NC):
                    store(it, c)

        @block.vector
        def _(dve):
            for s in (bound_part, bound_ready, stats_done, moments, normed, qk_low, v_copied, masked,
                      max_done, recip_done, attT_ready, att_added, x_low, h_high, h_low, ffn_added,
                      diffed, loss_out, best_loss, expert_found, y_ready):
                s.prime(dve)
            for z in (wd2s, bqk, bvb):
                nc.vector.memset(z[:], 0.0).then_inc(zeros_set, 1)
            nc.vector.memset(v2[:], 0.0).then_inc(quant, 1)
            nc.vector.memset(aT[R:R + 2, :], 1.0).then_inc(consts_ready, 1)
            dve.wait_ge(ffn_w_loaded, 32)
            n = 1
            for w, ld in enumerate((w1_ld, w2_ld)):
                nc.vector.tensor_reduce(gam[:, w:w + 1], ld, AX.X, ALU.add, apply_absolute_value=True)\
                    .then_inc(gamma_part, 1)
            for w, (ld, dst) in enumerate(((w1_ld, w1q), (w2_ld, w2q))):
                dve.wait_ge(gamma_sum, w + 1)
                nc.vector.tensor_scalar(gam[:, 4 + w:5 + w], gam[:, 2 + w:3 + w], 1.0 / (F * D), EPS, ALU.mult,
                                        ALU.add).then_inc(quant, 1)
                n += 1
                dve.wait_ge(quant, n)
                nc.vector.reciprocal(gam[:, 6 + w:7 + w], gam[:, 4 + w:5 + w]).then_inc(quant, 1)
                n += 1
                dve.wait_ge(quant, n)
                nc.vector.tensor_scalar(ld, ld, gam[:, 6 + w:7 + w], ROUND, ALU.mult, ALU.add).then_inc(quant, 1)
                n += 1
                dve.wait_ge(quant, n)
                nc.vector.tensor_scalar(ld, ld, ROUND, 1.0, ALU.subtract, ALU.min).then_inc(quant, 1)
                n += 1
                dve.wait_ge(quant, n)
                nc.vector.tensor_scalar(dst[:].rearrange("p k n -> p (k n)"), ld, -1.0, None, ALU.max)\
                    .then_inc(quant, 1)
                n += 1
            dve.wait_ge(quant, n)
            nc.vector.memset(kst[:].rearrange("p c r s k t -> p (c r s k t)").bitcast(F32), 0.0).then_inc(quant, 1)
            dve.wait_ge(w_loaded, 16 * N_W)
            nc.vector.tensor_copy(lens_f[:], lens_i[:]).then_inc(quant, 1)
            dve.wait_ge(quant, n + 2)
            dve.wait_ge(consts_ready, 7)

            def statistics(it, s, b):
                n = s * IB + b
                c = b // CB
                if s == 4:
                    src = x_ld
                    dve.wait_ge(x_loaded, it * 16 + 32)
                else:
                    src = xr
                    if s == 2:
                        ffn_added.done(dve, it, c)
                    else:
                        att_added.done(dve, it, IB * (s // 2) + b)
                moments.slot(dve, it, n, IB)
                nc.vector.bn_stats(stats[:, b], src[:, b, :]).then_inc(stats_done.sem, 1)

            def aggregate(it, s, b):
                n = s * IB + b
                stats_done.done(dve, it, n)
                normed.slot(dve, it, n, IB)
                carry(dve, dve_tally)
                nc.vector.bn_aggr(mv[:, b], stats[:, b]).then_inc(moments.sem, 1)

            def normalise(it, s, c):
                rstd_ready.done(dve, it, s * NC + c)
                xT_ready.slot(dve, it, s * NC + c, NC)
                for b in range(CB):
                    src = (x_ld if s == 4 else xr)[:, c * CB + b, :]
                    k = c * CB + b
                    nc.vector.tensor_scalar(xn[c][:, b], src, mv[:, k, 0:1], rstd[:, k:k + 1], ALU.subtract,
                                            ALU.mult).then_inc(normed.sem, 1)

            def low_parts(it, l, c, j):
                src = S[0] if j else S[1]
                for m in range(KD):
                    qk_high.done(dve, it, part_index(l, c, j, m))
                    nc.vector.scalar_tensor_tensor(out=packed[:, c, j, 1, m], in0=src[:, m * CT:m * CT + CT],
                                                   scalar=bqk[:, l % 2, j, m:m + 1], in1=packed[:, c, j, 0, m],
                                                   op0=ALU.add, op1=ALU.subtract).then_inc(qk_low.sem, 1)

            def values(it, l, c):
                v_ready.done(dve, it, 2 * l + c)
                mixed_ready.slot(dve, it, l * IB + c * CB + CB - 1, IB)
                for b in range(CB):
                    nc.vector.tensor_tensor(v2[:, c, b, :, 0:4:3, :],
                                            S[1][:, b * D:b * D + D].rearrange("p (a s d) -> p a s d", a=PAIRS, s=2),
                                            bvb[:, l].rearrange("p (a s d) -> p a s d", a=PAIRS, s=2),
                                            ALU.add).then_inc(v_copied.sem, 1)

            def attention(it, l):
                for t in range(UNITS + 10):
                    if l == 0 and t in EARLY_K:
                        low_parts(it, 1, EARLY_K.index(t), 1)
                    b1_, b2_, b3_ = t - 6, t - 9, t - 10
                    if t < UNITS:
                        g = UNITS * l + t
                        scores_ready.done(dve, it, g)
                        if t == 0:
                            bound_ready.done(dve, it, l)
                        if g >= 4:
                            probsT_ready.done(dve, it, 2 * (g - 4) + 1)
                        elif g < 2:
                            ctxT_ready.done(dve, it, NC - 1)
                        else:
                            bias_added.done(dve, it, NC - 1)
                            normed.done(dve, it, IB - 1)
                        nc.vector.tensor_tensor(sm[:, g % 4], S[t % 2][:].rearrange("p (h t) -> p h t", t=P),
                                                bound[:, l, t // 2].unsqueeze(1).to_broadcast([P, UH, P]),
                                                ALU.min).then_inc(masked.sem, 1)
                        masked.done(dve, it, g)
                        shifted.slot(dve, it, g, 4)
                        nc.vector.reduce_max(mx[:, g % 4], sm[:, g % 4], AX.X).then_inc(max_done.sem, 1)
                    if b1_ >= 0 and b1_ % 2 == 0 and b1_ // 2 < IB:
                        g = l * IB + b1_ // 2
                        mixed_copied.done(dve, it, g)
                        den = mixed[:, g % 2, 2 * P:4 * P]
                        nc.vector.reciprocal(den, den).then_inc(recip_done.sem, 1)
                        recip_done.done(dve, it, g)
                        nc.vector.tensor_tensor(attT[:, g % 2], attT[:, g % 2], den, ALU.mult)\
                            .then_inc(attT_ready.sem, 1)
                    if b2_ >= 0 and b2_ % 2 == 0 and b2_ // 2 < IB:
                        b = b2_ // 2
                        g = l * IB + b
                        oproj_ready.done(dve, it, g)
                        if l == 0:
                            bias_added.done(dve, it, b // CB)
                        nc.vector.tensor_tensor(xr[:, b], O[:, 0:D], xr[:, b], ALU.add).then_inc(att_added.sem, 1)
                    if b3_ >= 0 and b3_ % 2 == 0 and b3_ // 2 < IB:
                        statistics(it, 2 * l + 1, b3_ // 2)
                    if t - 11 >= 0 and t % 2 == 1 and (t - 11) // 2 < IB:
                        aggregate(it, 2 * l + 1, (t - 11) // 2)
                    if t == 19:
                        normalise(it, 2 * l + 1, 0)
                normalise(it, 2 * l + 1, 1)

            def bounds(it):
                scores_ready.past(dve, it, 2 * UNITS - 1)
                masked.past(dve, it, 2 * UNITS - 1)
                dve.wait_ge(mask_loaded, it * 16 + 16)
                nc.vector.tensor_scalar(bound[:, 0], mask_ld, 0.0, HUGE, ALU.not_equal, ALU.mult)\
                    .then_inc(bound_part.sem, 1)
                for b in range(IB):
                    ins = nc.vector.tensor_scalar(bound[:, 1, b], kpos[:], lens_f[:, bass.ds(it * IB + b, 1)], HUGE, ALU.is_lt,
                                                  ALU.mult)
                ins.then_inc(bound_part.sem, 1)
                bound_part.done(dve, it, 0)
                nc.vector.tensor_scalar(bound[:, 0], bound[:, 0], FILL[0], None, ALU.add)\
                    .then_inc(bound_ready.sem, 1)
                bound_part.done(dve, it, 1)
                nc.vector.tensor_scalar(bound[:, 1], bound[:, 1], FILL[1], None, ALU.add)\
                    .then_inc(bound_ready.sem, 1)

            def next_moments(it):
                for c in range(NC):
                    for b in range(CB):
                        statistics(it, 4, c * CB + b)
                    for b in range(CB):
                        aggregate(it, 4, c * CB + b)

            next_moments(-1)
            for c in range(NC):
                normalise(-1, 4, c)
            for c in range(NC):
                low_parts(-1, 2, c, 1)
            with dve.Fori(0, ITERS) as it:
                for l in range(2):
                    if l:
                        for c in range(NC):
                            normalise(it, 2, c)
                    for c in range(NC):
                        low_parts(it, l, c, 0)
                        values(it, l, c)
                    if l == 0:
                        bounds(it)
                    attention(it, l)
                    if l == 0:
                        for c in range(NC):
                            xT_copied.done(dve, it, NC + c)
                            nc.vector.tensor_tensor(xs16[c][:, 1].rearrange("p k t -> p (k t)"), S[0][:],
                                                    xs16[c][:, 0].rearrange("p k t -> p (k t)"),
                                                    ALU.subtract).then_inc(x_low.sem, 1)
                            if c == 0:
                                scores_ready.done(dve, it, UNITS - 1)
                            else:
                                for k in range(NC):
                                    dve.wait_ge(stacked[k], (it * 2 + 1) * STACK + (STACK_K + 16))
                            for j in range(KF // 2):
                                h_relu.done(dve, it, KF * c + 2 * j + 1)
                                nc.vector.tensor_copy(hh[c][:, 2 * j:2 * j + 2], work[:, j % 2])\
                                    .then_inc(h_high.sem, 1)
                                h_high.done(dve, it, 4 * c + j)
                                nc.vector.tensor_tensor(hl[c][:, 2 * j:2 * j + 2], work[:, j % 2],
                                                        hh[c][:, 2 * j:2 * j + 2], ALU.subtract)\
                                    .then_inc(h_low.sem, 1)
                        for c in range(NC):
                            ffn_ready.done(dve, it, c)
                            bias_added.done(dve, it, NC + c)
                            blk = xr[:, c * CB:c * CB + CB].rearrange("p b d -> p (b d)")
                            nc.vector.tensor_tensor(blk, S[1][:], blk, ALU.add).then_inc(ffn_added.sem, 1)
                            for b in range(CB):
                                statistics(it, 2, c * CB + b)
                            for b in range(CB):
                                aggregate(it, 2, c * CB + b)

                def choose(c):
                    loss_ready.done(dve, it, c)
                    k = c * CB * E
                    best_loss.past(dve, it, NC * CB - 1)
                    nc.vector.tensor_scalar(lneg[:, k:k + CB * E], V[0:1, 0:CB * E], -1.0, None, ALU.mult)\
                        .then_inc(loss_out.sem, 1)
                    loss_out.done(dve, it, c)
                    carry(dve, dve_tally)
                    for b in range(CB):
                        nc.vector.max(lmax[:, c * CB + b], lneg[:, k + b * E:k + b * E + E])\
                            .then_inc(best_loss.sem, 1)
                    for b in range(CB):
                        best_loss.done(dve, it, c * CB + b)
                        carry(dve, dve_tally)
                        nc.vector.max_index(lidx[:, c * CB + b], lmax[:, c * CB + b],
                                            lneg[:, k + b * E:k + b * E + E]).then_inc(expert_found.sem, 1)

                for c in range(NC):
                    xT_copied.done(dve, it, 3 * NC + c)
                    for e in range(E):
                        n = E * c + e
                        recon_ready.done(dve, it, n)
                        if n >= 2:
                            squared.done(dve, it, CB * (n - 1) - 1)
                        else:
                            h_low.done(dve, it, KF - 1)
                        for k in range(KD):
                            nc.vector.scalar_tensor_tensor(
                                out=work[:, e % 2, k], in0=S[(e + 1) % 2][:, k * CT:k * CT + CT],
                                scalar=bd2s[:, e, k:k + 1], in1=xT[c][:, k], op0=ALU.add,
                                op1=ALU.subtract).then_inc(diffed.sem, 1)
                        if c == 0 and e == E - 1:
                            next_moments(it)
                        if c == 1 and e == 1:
                            choose(0)
                        if c == 1 and e == 3:
                            for n in range(NC):
                                normalise(it, 4, n)
                choose(1)
                for c in range(NC):
                    low_parts(it, 2, c, 1)
                for c in range(NC):
                    up_ready.done(dve, it, c)
                    blk = xr[:, c * CB:c * CB + CB].rearrange("p b d -> p (b d)")
                    nc.vector.tensor_tensor(blk, S[c][:], blk, ALU.add).then_inc(y_ready.sem, 1)

        @block.tensor
        def _(pe):
            for s in (ctxT_ready, xT_ready, q_ready, k_ready, v_ready, scores_ready, probsT_ready,
                      mixed_ready, oproj_ready, h_ready, ffn_ready, hd_ready, recon_ready, loss_ready,
                      down_ready, up_ready):
                s.prime(pe)
            pe.wait_ge(w_loaded, 16 * N_W)
            pe.wait_ge(consts_ready, 7)
            pe.wait_ge(quant, 13)

            reader = {"S0": (y_ready, 0), "S1": (y_ready, 1), "T0": (a_relu, CB - 1), "T1": (a_relu, 2 * CB - 1),
                      "V": (loss_out, 1), "O": (att_added, 2 * IB - 1)}
            first = dict(reader)
            seen = set()

            def claim(it, tile, signal_, n):
                sig, m = reader[tile]
                if tile in seen:
                    sig.done(pe, it, m)
                else:
                    sig.past(pe, it, m)
                seen.add(tile)
                reader[tile] = (signal_, n)

            def flip(it, dst, src, last):
                for k in range(KD):
                    for b in range(CB):
                        ins = nc.tensor.transpose(dst[:, k * CT + b * P:k * CT + b * P + P],
                                                  src[:, b, k * P:k * P + P], ident[:])
                ins.then_inc(last.sem, 1)

            def transpose_x(it, s, c):
                claim(it, "S0", *((x_low, c) if s == 1 else (xT_copied, s * NC + c)))
                normed.done(pe, it, s * IB + c * CB + CB - 1)
                flip(it, S[0], xn[c], xT_ready)

            def project(dst, w, src, last):
                for m in range(KD):
                    for k in range(KD):
                        ins = nc.tensor.matmul(dst[:, m * CT:m * CT + CT], w[:, k, m * P:m * P + P], src[:, k],
                                               start=(k == 0), stop=(k == KD - 1))
                ins.then_inc(last.sem, 1)

            def project_k(it, l, c):
                claim(it, "S0", qk_low, part_index(l, c, 1, KD - 1))
                project(S[0], wk[l % 2], ctxT[:, c], k_ready)

            def next_keys(it):
                pe.wait_ge(ctx_loaded, it * 16 + 32)
                for c in range(NC):
                    claim(it, f"S{c}", ctxT_copied, NC + c)
                    flip(it, S[c], ctx_ld[:, c * CB:c * CB + CB], ctxT_ready)
                for c in range(NC):
                    ctxT_copied.done(pe, it, NC + c)
                    project_k(it, 2, c)

            def attention(it, l):
                def scores(u):
                    g = UNITS * l + u
                    b, c = u // 2, u // 8
                    claim(it, f"S{u % 2}", masked, g)
                    if u % 8 == 0:
                        pe.wait_ge(stacked[c], (it * 2 + l + 1) * STACK + 16)
                    t0 = (b % CB) * P
                    for a in range(4):
                        ins = nc.tensor.matmul(
                            S[u % 2][:, a * 2 * P:a * 2 * P + 2 * P], qst[:, c, a, u % 2, t0:t0 + P],
                            kst[:, c, a, :, u % 2, t0:t0 + P], start=True, stop=True)
                    ins.then_inc(scores_ready.sem, 1)

                def transposes(u):
                    g = UNITS * l + u
                    exp_done.done(pe, it, g)
                    for q in range(2):
                        claim(it, f"T{q}", probsT_copied, 2 * g + q)
                        for h in range(4):
                            ins = nc.tensor.transpose(T[q][:, h * P:h * P + P], sm[:, g % 4, 4 * q + h], ident[:])
                        ins.then_inc(probsT_ready.sem, 1)

                def mix(u):
                    g = UNITS * l + u
                    b, half = u // 2, u % 2
                    c = b // CB
                    if half == 0:
                        claim(it, "V", mixed_copied, l * IB + b)
                        v_copied.done(pe, it, l * IB + b)
                    probsT_copied.done(pe, it, 2 * g + 1)
                    for part in range(2):
                        for s in range(2):
                            for a in range(4):
                                pair = 4 * half + a
                                w = v2[:, c, b % CB, pair, 2 * s:2 * s + 2] if part == 0 else sel[:, s]
                                if part == 0:
                                    w = w.rearrange("p s d -> p (s d)")
                                ins = nc.tensor.matmul(
                                    V[32 * a:32 * a + 32, (2 * part + half) * P:(2 * part + half) * P + P], w,
                                    pT[:, half, 2 * a + s], start=(s == 0), stop=(s == 1))
                    if half:
                        ins.then_inc(mixed_ready.sem, 1)

                def output(b):
                    g = l * IB + b
                    claim(it, "O", att_added, g)
                    attT_ready.done(pe, it, g)
                    for k in range(KD):
                        ins = nc.tensor.matmul(O[:, 0:D], attT[:, g % 2, k * P:k * P + P], wo[l][:, k],
                                               start=(k == 0), stop=(k == KD - 1))
                    ins.then_inc(oproj_ready.sem, 1)

                for t in range(UNITS + LAG + 5):
                    if l == 0 and t in EARLY_K:
                        project_k(it, 1, EARLY_K.index(t))
                    if t < UNITS:
                        scores(t)
                    if LAG <= t < UNITS + LAG:
                        transposes(t - LAG)
                    if LAG + 1 <= t < UNITS + LAG + 1:
                        mix(t - LAG - 1)
                    if t >= 8 and t % 2 == 0 and (t - 8) // 2 < IB:
                        output((t - 8) // 2)

            next_keys(-1)
            qk_low.done(pe, -1, part_index(2, NC - 1, 1, KD - 1))
            ctxT_copied.done(pe, -1, 2 * NC - 1)
            reader.update(first)
            seen.clear()
            with pe.Fori(0, ITERS) as it:
                for l in range(2):
                    for c in range(NC):
                        transpose_x(it, 2 * l, c)
                        claim(it, "S1", qk_low, part_index(l, c, 0, KD - 1))
                        xT_copied.done(pe, it, 2 * l * NC + c)
                        project(S[1], wq[l], xT[c], q_ready)
                        if l == 0:
                            ctxT_copied.done(pe, it, c)
                        claim(it, "S1", v_copied, l * IB + c * CB + CB - 1)
                        for b in range(CB):
                            for k in range(KD):
                                ins = nc.tensor.matmul(S[1][:, b * D:b * D + D], ctxT[:, c, k, b * P:b * P + P],
                                                       wv[l][:, k], start=(k == 0), stop=(k == KD - 1))
                        ins.then_inc(v_ready.sem, 1)
                    attention(it, l)
                    if l == 0:
                        for c in range(NC):
                            transpose_x(it, 1, c)
                            x_low.done(pe, it, c)
                            for j in range(KF // 2):
                                claim(it, f"S{(j + 1) % 2}", h_relu, KF * c + 2 * j + 1)
                                for m in range(2):
                                    f0 = (2 * j + m) * P
                                    for n in range(2 * KD):
                                        k, part = n // 2, n % 2
                                        ins = nc.tensor.matmul(S[(j + 1) % 2][:, m * CT:m * CT + CT],
                                                               w1q[:, k, f0:f0 + P], xs16[c][:, part, k],
                                                               start=(n == 0), stop=(n == 2 * KD - 1))
                                ins.then_inc(h_ready.sem, 1)
                        for c in range(NC):
                            claim(it, "S1", ffn_added, c)
                            h_low.done(pe, it, 4 * c + 3)
                            for b in range(CB):
                                for n in range(2 * KF):
                                    k, part = n // 2, (hh, hl)[n % 2][c]
                                    ins = nc.tensor.matmul(S[1][:, b * D:b * D + D], part[:, k, b * P:b * P + P],
                                                           w2q[:, k], start=(n == 0), stop=(n == 2 * KF - 1))
                            ins.then_inc(ffn_ready.sem, 1)
                for c in range(NC):
                    transpose_x(it, 3, c)
                    xT_copied.done(pe, it, 3 * NC + c)
                    for j in range(2):
                        claim(it, f"S{(j + 1) % 2}", hd_relu, 4 * c + 2 * j + 1)
                        for m in range(2):
                            e0 = 2 * (2 * j + m)
                            for k in range(KD):
                                ins = nc.tensor.matmul(S[(j + 1) % 2][:, m * CT:m * CT + CT],
                                                       wd1s[:, k, e0:e0 + 2].rearrange("p e r -> p (e r)"),
                                                       xT[c][:, k], start=(k == 0), stop=(k == KD - 1))
                        ins.then_inc(hd_ready.sem, 1)
                    for e in range(E):
                        claim(it, f"S{(e + 1) % 2}", diffed, (E * c + e) * KD + 1)
                        hd_relu.done(pe, it, 4 * c + e // 2)
                        for m in range(KD):
                            ins = nc.tensor.matmul(S[(e + 1) % 2][:, m * CT:m * CT + CT],
                                                   wd2s[:, e, m * P:m * P + P], hd[c][:, e // 2],
                                                   start=True, stop=True)
                        ins.then_inc(recon_ready.sem, 1)
                    claim(it, "V", loss_out, c)
                    squared.done(pe, it, CB * E * (c + 1) - 1)
                    nc.tensor.matmul(V[0:1, 0:CB * E], ones[:], acc[:, CB * E * c:CB * E * c + CB * E],
                                     start=True, stop=True).then_inc(loss_ready.sem, 1)
                next_keys(it)
                for c in range(NC):
                    pe.wait_ge(gathered[c], it * GATHER + GATHER)
                    claim(it, f"T{c}", a_relu, c * CB + CB - 1)
                    for b in range(CB):
                        for k in range(KD):
                            ins = nc.tensor.matmul(T[c][0:R, b * P:b * P + P], adapter[c][b][:, k * R:k * R + R], xT[c][:, k, b * P:b * P + P],
                                                   start=(k == 0), stop=(k == KD - 1))
                    ins.then_inc(down_ready.sem, 1)
                    claim(it, f"S{c}", y_ready, c)
                    for b in range(CB):
                        for k in range(KD):
                            nc.tensor.matmul(S[c][:, b * D:b * D + D], xT[c][:, k, b * P:b * P + P], wb[:, k],
                                             start=(k == 0), stop=False)
                        a_relu.done(pe, it, c * CB + b)
                        ins = nc.tensor.matmul(S[c][:, b * D:b * D + D], aT[:, b * P:b * P + P], adapter[c][b][0:R + 2, KD * R:KD * R + D],
                                               start=False, stop=True)
                    ins.then_inc(up_ready.sem, 1)
            assert reader == first, reader


_ARGS = [
    ("x", "x"), ("ctx", "ctx_1024"), ("lens", "_lenS2"), ("mask", "mask_Bx1xSxS2_if1"),
    ("wq0", "L0_xattn_w_q"), ("bq0", "L0_xattn_b_q"), ("wk0", "L0_xattn_w_k"), ("bk0", "L0_xattn_b_k"),
    ("wv0", "L0_xattn_w_v"), ("bv0", "L0_xattn_b_v"), ("wo0", "L0_xattn_w_o"), ("bo0", "L0_xattn_b_o"),
    ("w1t", "L0_ffn_W1"), ("b1", "L0_ffn_b1"), ("w2t", "L0_ffn_W2"), ("b2", "L0_ffn_b2"),
    ("wq1", "L1_xattn_W_q"), ("wk1", "L1_xattn_W_k"), ("wv1", "L1_xattn_W_v"), ("wo1", "L1_xattn_W_o"),
    ("w_base", "L1_ffn_W_base"), ("wd1", "L1_ffn_Wd1"), ("bd1", "L1_ffn_bd1"),
    ("wd2", "L1_ffn_Wd2"), ("bd2", "L1_ffn_bd2"),
]
_TRANSPOSED = {"w1t", "w2t", "wq1", "wk1", "wv1", "wo1"}


def lay_out_adapters(wa_down, wa_up, ba_up, b_base, ba_down):
    a = np.zeros((E, P, AW), np.float32)
    for k in range(KD):
        a[:, :, k * R:k * R + R] = wa_down[:, k * P:k * P + P, :]
    a[:, 0:R, KD * R:KD * R + D] = wa_up
    a[:, R, KD * R:KD * R + D] = ba_up
    a[:, R + 1, KD * R:KD * R + D] = b_base
    a[:, 0:R, AW - 1] = ba_down
    return a


def kernel(**inputs):
    import concourse.bacc as bacc
    from concourse.bass_utils import run_bass_kernel_spmd

    nc = bacc.Bacc("TRN2", target_bir_lowering=False, num_devices=1)
    arrays, args = {}, []
    for name, key in _ARGS:
        a = np.asarray(inputs[key])
        a = np.ascontiguousarray(a.T if name in _TRANSPOSED else a)
        arrays[f"in_{name}"] = a
        args.append(nc.dram_tensor(f"in_{name}", a.shape, mybir.dt.from_np(a.dtype), kind="ExternalInput").ap())
    a = lay_out_adapters(*(np.asarray(inputs["L1_ffn_" + k]) for k in (
        "Wa_down", "Wa_up", "ba_up", "b_base", "ba_down")))
    arrays["in_adapters"] = a
    args.append(nc.dram_tensor("in_adapters", a.shape, F32, kind="ExternalInput").ap())
    y = nc.dram_tensor("out_y", (B, P, D), F32, kind="ExternalOutput").ap()
    nc.disable_value_cache = True
    build(nc, *args, y)
    r = run_bass_kernel_spmd(nc, [arrays], core_ids=[0])
    return r.results[0]["out_y"]
```
